# Optimizing a Trainium2 kernel written in Bass

```python
import numpy as np
import jax
import jax.numpy as jnp

def _softmax(x, axis=-1):
    return jax.nn.softmax(x, axis=axis)

def _gelu(x):
    return jax.nn.gelu(x, approximate=True)

def _silu(x):
    return jax.nn.silu(x)

def _sigmoid(x):
    return jax.nn.sigmoid(x)

def _layernorm(x, axis=-1, eps=1e-05):
    m = jnp.mean(x, axis=axis, keepdims=True)
    v = jnp.var(x, axis=axis, keepdims=True)
    return (x - m) / jnp.sqrt(v + eps)

def _scatter_add(tgt, idx, src, axis=0):
    return tgt.at[idx].add(src)

def _segment_sum(src, seg, n):
    return jax.ops.segment_sum(src, seg, n)
kernel_name = 'mk_adj_resnorm_d4_adj_r2_609c71'

def setup_inputs(seed: int=0):
    np.random.seed(seed)
    _w = jnp.asarray

    def _rec_inputs():
        import jax
        import jax.numpy as jnp
        _gk = jax.random.key(seed)
        x = -0.000929 + 1 * jax.random.normal(jax.random.fold_in(_gk, 1), (4096, 64), jnp.float32)
        _a = jax.random.bernoulli(jax.random.fold_in(_gk, 2), 0.00390625, (4096, 4096))
        _a = jnp.logical_or(_a, jnp.eye(4096, dtype=bool))
        _af = _a.astype(jnp.float32)
        _af = _af * jax.random.uniform(jax.random.fold_in(_gk, 3), (4096, 4096), jnp.float32, 0.05, 1)
        adj = _af
        return (x, adj)
    x, adj = _rec_inputs()

    def _L0_gnn_setup():
        import jax, jax.numpy as jnp
        import numpy as np
        HOP = 2
        N = 8192
        HIDDEN = 64
        key = jax.random.key(seed)
        k1, k2, k3 = jax.random.split(key, 3)
        user_embs = jax.random.normal(k1, (N, HIDDEN), dtype=jnp.float32)
        adj = jax.random.uniform(k2, (N, N), dtype=jnp.float32)
        limit = float(np.sqrt(6.0 / (2 * HIDDEN + HIDDEN)))
        W = jax.random.uniform(k3, (HOP, 2 * HIDDEN, HIDDEN), dtype=jnp.float32, minval=-limit, maxval=limit)
        return {'user_embs': user_embs, 'adj': adj, 'W': W}
    _L0_gnn_all = _L0_gnn_setup()
    _L0_gnn_in = {k: v for k, v in _L0_gnn_all.items() if k in ('W',)}
    del _L0_gnn_all

    def _L1_gnn_setup():
        import jax, jax.numpy as jnp
        import numpy as np
        N = 8192
        F_IN = 64
        F_OUT = 64
        key = jax.random.key(seed)
        k1, k2, k3 = jax.random.split(key, 3)
        x = jax.random.normal(k1, (N, F_IN), dtype=jnp.float32)
        adj = jax.random.randint(k2, (N, N), 0, 2).astype(jnp.float32)
        W = jax.random.normal(k3, (F_IN, F_OUT), dtype=jnp.float32) * (1.0 / np.sqrt(F_IN))
        b = jnp.zeros((F_OUT,), dtype=jnp.float32)
        return {'x': x, 'adj': adj, 'W': W, 'b': b}
    _L1_gnn_all = _L1_gnn_setup()
    _L1_gnn_in = {k: v for k, v in _L1_gnn_all.items() if k in ('W', 'b')}
    del _L1_gnn_all

    def _L2_gnn_setup():
        import jax, jax.numpy as jnp
        import numpy as np
        N = 4096
        F_IN = 64
        F_OUT = 64
        K = 4
        key = jax.random.key(seed)
        k1, k2, k3 = jax.random.split(key, 3)
        x = jax.random.normal(k1, (N, F_IN), dtype=jnp.float32)
        L = jax.random.normal(k2, (N, N), dtype=jnp.float32) * (1.0 / np.sqrt(N))
        weight = jax.random.normal(k3, (K, F_IN, F_OUT), dtype=jnp.float32) * (1.0 / np.sqrt(F_IN))
        return {'x': x, 'L': L, 'weight': weight}
    _L2_gnn_all = _L2_gnn_setup()
    _L2_gnn_in = {k: v for k, v in _L2_gnn_all.items() if k in ('weight',)}
    del _L2_gnn_all

    def _L3_gnn_setup():
        import jax, jax.numpy as jnp
        import numpy as np
        N = 2048
        F = 64
        H = 8
        D = 8
        key = jax.random.key(seed)
        k1, k2, k3, k4, k5, k6 = jax.random.split(key, 6)
        X = jax.random.normal(k1, (N, F), dtype=jnp.float32)
        A = (jax.random.uniform(k2, (N, N)) < 0.01).astype(jnp.float32)
        A = jnp.maximum(A, jnp.eye(N, dtype=jnp.float32))
        lim_w = np.sqrt(6.0 / (F + H * D)).astype(np.float32)
        W = jax.random.uniform(k3, (F, H * D), minval=-lim_w, maxval=lim_w, dtype=jnp.float32)
        lim_a = np.sqrt(6.0 / (1 + H * D)).astype(np.float32)
        att_self = jax.random.uniform(k4, (H, D), minval=-lim_a, maxval=lim_a, dtype=jnp.float32)
        att_neigh = jax.random.uniform(k5, (H, D), minval=-lim_a, maxval=lim_a, dtype=jnp.float32)
        bias = jnp.zeros((H, D), dtype=jnp.float32)
        return {'X': X, 'A': A, 'W': W, 'att_self': att_self, 'att_neigh': att_neigh, 'bias': bias}
    _L3_gnn_all = _L3_gnn_setup()
    _L3_gnn_in = {k: v for k, v in _L3_gnn_all.items() if k in ('W', 'att_self', 'att_neigh', 'bias')}
    del _L3_gnn_all
    return {'x': x, 'adj': adj, 'L0_gnn_W': _L0_gnn_in['W'], 'L1_gnn_W': _L1_gnn_in['W'], 'L1_gnn_b': _L1_gnn_in['b'], 'L2_gnn_weight': _L2_gnn_in['weight'], 'L3_gnn_W': _L3_gnn_in['W'], 'L3_gnn_att_self': _L3_gnn_in['att_self'], 'L3_gnn_att_neigh': _L3_gnn_in['att_neigh'], 'L3_gnn_bias': _L3_gnn_in['bias']}

def reference(x, adj, L0_gnn_W, L1_gnn_W, L1_gnn_b, L2_gnn_weight, L3_gnn_W, L3_gnn_att_self, L3_gnn_att_neigh, L3_gnn_bias):
    import jax
    import jax.numpy as jnp

    def _L0_gnn_ref(user_embs, adj, W):
        import jax, jax.numpy as jnp
        import numpy as np
        HOP = 2
        N = 8192
        HIDDEN = 64
        x = user_embs
        for k in range(HOP):
            agg = adj @ x
            x = jnp.tanh(jnp.concatenate([agg, x], axis=1) @ W[k])
        return x

    def _L1_gnn_ref(x, adj, W, b):
        import jax, jax.numpy as jnp
        import numpy as np
        N = 8192
        F_IN = 64
        F_OUT = 64
        deg = adj.sum(axis=0) + 1.0
        dinv = jnp.where(deg > 0, jax.lax.rsqrt(deg), 0.0)
        xw = x @ W
        z = dinv[:, None] * xw
        out = dinv[:, None] * (adj.T @ z + z) + b
        return jax.nn.relu(out)

    def _L2_gnn_ref(x, L, weight):
        import jax, jax.numpy as jnp
        import numpy as np
        N = 4096
        F_IN = 64
        F_OUT = 64
        K = 4
        terms = [x, L @ x]
        for _ in range(2, K):
            terms.append(2.0 * (L @ terms[-1]) - terms[-2])
        feature = jnp.stack(terms, axis=0)
        return jnp.einsum('kni,kio->no', feature, weight)

    def _L3_gnn_ref(X, A, W, att_self, att_neigh, bias):
        import jax, jax.numpy as jnp
        import numpy as np
        N = 2048
        F = 64
        H = 8
        D = 8
        feats = (X @ W).reshape(-1, H, D)
        a_self = jnp.einsum('nhd,hd->nh', feats, att_self)
        a_neigh = jnp.einsum('nhd,hd->nh', feats, att_neigh)
        scores = a_self.T[:, :, None] + a_neigh.T[:, None, :]
        scores = jax.nn.leaky_relu(scores, negative_slope=0.2)
        scores = scores + (-10000000000.0 * (1.0 - A))[None, :, :]
        attn = jax.nn.softmax(scores, axis=-1)
        out = jnp.einsum('hij,jhd->ihd', attn, feats)
        out = out + bias[None, :, :]
        out = out.reshape(-1, H * D)
        return jax.nn.relu(out)
    x = _layernorm(x + _L0_gnn_ref(x, adj, L0_gnn_W), axis=-1)
    x = _layernorm(x + _L1_gnn_ref(x, adj, L1_gnn_W, L1_gnn_b), axis=-1)
    x = _layernorm(x + _L2_gnn_ref(x, adj, L2_gnn_weight), axis=-1)
    x = _layernorm(x + _L3_gnn_ref(x, adj, L3_gnn_W, L3_gnn_att_self, L3_gnn_att_neigh, L3_gnn_bias), axis=-1)
    return x

_drawn_inputs = setup_inputs


def setup_inputs(seed=0):
    import zlib

    import numpy as np

    out = dict(_drawn_inputs(seed))
    spreads = {'L1_gnn_b': (0.0, 0.1), 'L3_gnn_bias': (0.0, 0.1)}
    factors = {}
    for name, (base, spread) in spreads.items():
        noise = np.random.default_rng([zlib.crc32(name.encode()), seed]).standard_normal(out[name].shape)
        drawn = base * np.exp(spread * noise) if base else spread * noise
        out[name] = jnp.asarray(drawn.astype(out[name].dtype))
    for name, factor in factors.items():
        out[name] = (out[name] * factor).astype(out[name].dtype)
    return out
```

```python
from contextlib import ExitStack

import concourse.bass as bass
from concourse import mybir

F32 = mybir.dt.float32
U32 = mybir.dt.uint32
I32 = mybir.dt.int32
ALU = mybir.AluOpType
ACT = mybir.ActivationFunctionType
X = mybir.AxisListType.X

P = 128
N, F = 4096, 64
H, D = 8, 8
BLOCKS = N // P
SB = 4
BPS = BLOCKS // SB
QUARTER = N // SB
HALF = QUARTER // 2
STEPS = BLOCKS
TURN_BUFS, TILE_BUFS = 2, 4
SCAN = 4
EPS = 1e-5
NEG = -1e10

HOP1, HOP2, SPREAD, CHEB1, CHEB2, CHEB3 = range(6)
TURNED = {HOP1: 0, HOP2: 1, CHEB1: 2, CHEB2: 3, CHEB3: 4}

W_H1A, W_H1X, W_H2A, W_H2X, W_GCN, W_C0, W_C1, W_C2, W_C3, W_GAT, W_ONE = range(11)


def superblock(stream, v):
    return v if stream % 2 == 0 else SB - 1 - v


def quarters(stream):
    return [3, 2, 1, 0] if stream == CHEB2 else [0, 1, 2, 3]


def loaded(stream, v):
    return 16 * (1 + (SB - 1) * stream + v)


def step_no(stream, v, pos):
    return STEPS * SB * TURNED[stream] + STEPS * v + pos


def rows_hop1(v):
    return 1 + v


def rows_hop2(v):
    return 5 + 2 * v


def rows_gcn(v):
    return 6 + 2 * v


def rows_spread(q):
    return 13 + q


def rows_cheb1(v):
    return 17 + v


def rows_cheb2(v):
    return 21 + v


def rows_gat(v):
    return 25 + v


def flip_hop1(v):
    return 1 + v


def flip_hop2(v):
    return 5 + 2 * v


def flip_gcn(v):
    return 6 + 2 * v


def flip_cheb1(v):
    return 13 + 2 * v


def filt_cheb1(v):
    return 14 + 2 * v


def filt_cheb2(v):
    return 21 + v


def filt_cheb3(v):
    return 25 + 2 * v


def flip_gat(v):
    return 26 + 2 * v


def wait_apart(eng, semaphore, value, holds):
    if isinstance(value, int):
        eng.wait_ge(semaphore, value)
        return
    value = eng.to_reg(value)
    eng.wait_ge(holds, 1)
    eng.wait_ge(semaphore, value)


def build(nc, x, adj, w_hop, w_gcn, b_gcn, w_cheb, w_gat, att_self, att_neigh, b_gat, out):
    ctx = ExitStack()
    with ctx:
        def sb(name, shape, dt=F32):
            return ctx.enter_context(nc.sbuf_tensor(name, shape, dt))

        def ps(name, shape):
            return ctx.enter_context(nc.psum_tensor(name, shape, F32))

        def sem(name):
            return ctx.enter_context(nc.semaphore(name))

        feats_dram = nc.dram_tensor("feats_scratch", [N, F], F32, kind="Internal")
        neigh_dram = nc.dram_tensor("neigh_scratch", [BLOCKS * H, P], F32, kind="Internal")

        ring = sb("ring", [P, SB, BPS, QUARTER])
        tiles = sb("tiles", [P, TILE_BUFS, QUARTER])
        buf_a = sb("buf_a", [P, BLOCKS, F])
        buf_b = sb("buf_b", [P, BLOCKS, F])
        buf_c = sb("buf_c", [P, BLOCKS, F])
        buf_d = sb("buf_d", [P, BLOCKS, F])
        x0 = y2 = buf_a
        hop = buf_b
        t2 = attended = buf_b
        y1 = t1 = y3 = buf_c
        z = filtered = feats = buf_d
        spread_sums = buf_b[:, :, :].rearrange("p b f -> p (b f)").rearrange("p (q n) -> p q n", q=SB)

        ident = sb("ident", [P, P])
        wb = sb("wb", [P, 11, P])
        per_row = sb("per_row", [P, 4, F])
        sums = sb("sums", [P, HALF])
        staged_rows = sb("staged_rows", [P, BPS, F])
        paired = sb("paired", [P, HALF])
        second_hop = sb("second_hop", [P, BPS, F])
        work = sb("work", [P, BPS, F])
        square = sb("square", [P, BPS, F])
        rowsum = sb("rowsum", [P, BPS])
        root_t = sb("root_t", [P, BLOCKS])
        root_y = sb("root_y", [P, BLOCKS])
        root_x = sb("root_x", [P, BLOCKS])
        deg_part = sb("deg_part", [P, BLOCKS])
        deg = sb("deg", [P, BLOCKS])
        dinv = sb("dinv", [P, BLOCKS])
        top8 = sb("top8", [P, SCAN, 8])
        top8_at = sb("top8_at", [P, SCAN, 8], U32)
        top2 = sb("top2", [P, BLOCKS, SB, 2])
        top_at = sb("top_at", [P, BLOCKS, SB])
        best = sb("best", [P, BLOCKS, 8])
        hit = sb("hit", [P, BLOCKS, SB])
        neighbour = sb("neighbour", [P, BLOCKS])
        neighbour_u = sb("neighbour_u", [P, BLOCKS], U32)
        lead = sb("lead", [P, 3, BLOCKS])
        att = sb("att", [P, 2, BLOCKS, H])
        worst = sb("worst", [P, 3])
        worst_all = sb("worst_all", [P, 3])
        verdict = sb("verdict", [P, 2])
        onehot = sb("onehot", [P, 1], I32)
        neg_max = sb("neg_max", [P, 4])
        weight_sum = sb("weight_sum", [P, 4])

        pe_turn = [ps(f"pe_turn{i}", [P, 2, HALF]) for i in range(TURN_BUFS)]
        pe_sum = ps("pe_sum", [P, HALF])
        pe_rows = ps("pe_rows", [P, BPS, F])
        pe_flip = ps("pe_flip", [P, BPS, F])

        chunk_loaded = [sem(f"chunk_loaded{q}") for q in range(SB)]
        x_loaded = sem("x_loaded")
        small_loaded = sem("small_loaded")
        consts_zeroed = sem("consts_zeroed")
        consts_ready = sem("consts_ready")
        turned = sem("turned")
        evacuated = sem("evacuated")
        multiplied = sem("multiplied")
        sums_copied = sem("sums_copied")
        rows_filled = sem("rows_filled")
        rows_read = sem("rows_read")
        flip_filled = sem("flip_filled")
        flip_read = sem("flip_read")
        staged = sem("staged")
        scanned = sem("scanned")
        deg_added = sem("deg_added")
        spread = sem("spread")
        spread_copied = sem("spread_copied")
        y2_ready = sem("y2_ready")
        vec = sem("vec")
        feats_stored = sem("feats_stored")
        worst_found = sem("worst_found")
        worst_reduced = sem("worst_reduced")
        verdict_ready = sem("verdict_ready")
        gathered = [sem(f"gathered{s}") for s in range(SB)]
        out_ready = sem("out_ready")
        out_stored = sem("out_stored")
        neigh_turned = sem("neigh_turned")
        neigh_copied = sem("neigh_copied")
        neigh_stored = sem("neigh_stored")
        neigh_loaded = sem("neigh_loaded")
        mask_loaded = sem("mask_loaded")
        scores_ready = sem("scores_ready")
        probs_ready = sem("probs_ready")
        probs_turned = sem("probs_turned")
        probs_copied = sem("probs_copied")
        heads_summed = sem("heads_summed")
        heads_read = sem("heads_read")

        adj_rows = adj.rearrange("(t p) j -> p t j", p=P)
        x_rows = x.rearrange("(t p) f -> p t f", p=P)
        out_rows = out.rearrange("(t p) f -> p t f", p=P)
        feats_rows = feats_dram[:, :].rearrange("(t p) f -> p t f", p=P)

        def rows_of(buf, s):
            return buf[:, bass.ds(s * BPS, BPS), :]

        def split(a):
            return a.rearrange("p (h t) f -> p h t f", h=2)

        def staged_by_half():
            return staged_rows[:, :, :].rearrange("p (t h) f -> p h t f", h=2)

        def pairs(t):
            return lambda a: a[:, t::BPS // 2, :]

        wb_loads = [(w_hop.rearrange("k (a f) g -> f (k a) g", a=2), W_H1A, 4),
                    (w_gcn.rearrange("f (k g) -> f k g", k=1), W_GCN, 1),
                    (w_cheb.rearrange("k f g -> f k g"), W_C0, 4),
                    (w_gat.rearrange("f (k g) -> f k g", k=1), W_GAT, 1)]
        rows_loads = [b_gcn, att_self.rearrange("h d -> (h d)"), att_neigh.rearrange("h d -> (h d)"),
                      b_gat.rearrange("h d -> (h d)")]

        flat_ring = ring[:, :, :, :].rearrange("p q t n -> p (q t n)")

        def neigh_terms(h):
            return flat_ring[:, h * N:(h + 1) * N]

        def mask():
            return flat_ring[:, 4 * N:5 * N]

        def scores():
            return flat_ring[:, 5 * N:6 * N]

        def probs():
            return flat_ring[:, 6 * N:7 * N]

        block = ctx.enter_context(nc.Block())

        @block.sync
        def _(sp):
            for q in range(SB):
                sp.dma_start(ring[:, q], adj_rows[:, 0:BPS, q * QUARTER:(q + 1) * QUARTER])\
                    .then_inc(chunk_loaded[q], 16)
                if q == 0:
                    sp.dma_start(x0[:, :, :], x_rows).then_inc(x_loaded, 16)

            def reload(stream, v):
                s = superblock(stream, v)
                for r, q in enumerate(quarters(stream)):
                    if stream == SPREAD:
                        wait_apart(sp, spread, SB * (v - 1) + r + 1, consts_zeroed)
                    else:
                        wait_apart(sp, turned, step_no(stream, v - 1, BPS * r) + BPS, consts_zeroed)
                    if stream in (HOP1, HOP2):
                        wait_apart(sp, scanned, SB * SB * stream + SB * (v - 1) + r + 1, consts_zeroed)
                    sp.dma_start(ring[:, q], adj_rows[:, bass.ds(s * BPS, BPS), q * QUARTER:(q + 1) * QUARTER])\
                        .then_inc(chunk_loaded[q], 16)

            for stream in range(6):
                if stream == SPREAD:
                    sp.wait_ge(scanned, 2 * SB * SB)
                with sp.Fori(1, SB) as v:
                    reload(stream, v)
            for v in range(SB):
                s = superblock(CHEB3, v)
                sp.wait_ge(rows_read, rows_gat(v) + 1)
                sp.dma_start(feats_rows[:, s * BPS:(s + 1) * BPS, :], rows_of(feats, s)).then_inc(feats_stored, 16)
            sp.wait_ge(feats_stored, 16 * SB)

            sp.wait_ge(verdict_ready, 1)
            one = sp.value_load(onehot[0:1, 0:1], min_val=0, max_val=1)
            with sp.If(one == 0):
                sp.wait_ge(neigh_copied, 1)
                sp.dma_start(neigh_dram[:, :].rearrange("(c b) p -> b c p", c=2),
                             staged_rows[:, :, :].rearrange("p b f -> p (b f)")[:, 0:2 * P]
                             .rearrange("p (c n) -> p c n", c=2)).then_inc(neigh_stored, 16)
                sp.wait_ge(neigh_stored, 16)
                neigh_all = neigh_dram[:, :].rearrange("(b h) p -> h b p", h=H)
                for g in range(2):
                    sp.wait_ge(heads_read, g * BLOCKS + 1)
                    for h in range(4):
                        sp.dma_start(neigh_terms(h).rearrange("p (b n) -> p b n", b=BLOCKS),
                                     neigh_all[4 * g + h].partition_broadcast(P)).then_inc(neigh_loaded, 16)
                    with sp.Fori(0, BLOCKS) as b:
                        wait_apart(sp, heads_read, b + (g * BLOCKS + 1), consts_zeroed)
                        sp.dma_start(mask(), adj[bass.ds(b * P, P), :]).then_inc(mask_loaded, 16)
                        wait_apart(sp, mask_loaded, b * 16 + (g * BLOCKS + 1) * 16, consts_zeroed)
            for s in range(SB):
                sp.wait_ge(out_ready, s + 1)
                sp.dma_start(out_rows[:, s * BPS:(s + 1) * BPS, :], rows_of(attended, s)).then_inc(out_stored, 16)
            sp.wait_ge(out_stored, 16 * SB)

        @block.gpsimd
        def _(pool):
            pool.memset(ident[:, :], 0.0).then_inc(consts_zeroed, 1)
            pool.memset(wb[:, :, :], 0.0).then_inc(consts_zeroed, 1)
            pool.memset(deg[:, :], 1.0).then_inc(consts_zeroed, 1)
            pool.memset(lead[:, 0, :], 0.0).then_inc(evacuated, TURN_BUFS)
            pool.memset(lead[:, 1, :], 0.0).then_inc(multiplied, TILE_BUFS)
            for i, count in enumerate((rows_filled, rows_read, flip_filled, flip_read, heads_read,
                                       probs_ready, probs_turned, probs_copied)):
                pool.memset(deg_part[:, i:i + 1], 0.0).then_inc(count, 1)
            pool.wait_ge(consts_zeroed, 2)
            pool.affine_select(out=ident[:, :], in_=ident[:, :], compare_op=ALU.not_equal, fill=1.0,
                               base=0, pattern=[[-1, P]], channel_multiplier=1).then_inc(consts_ready, 1)
            pool.affine_select(out=wb[:, W_ONE, :], in_=wb[:, W_ONE, :], compare_op=ALU.not_equal, fill=1.0,
                               base=0, pattern=[[-1, P]], channel_multiplier=1).then_inc(consts_ready, 1)
            pool.wait_ge(worst_found, 1)
            pool.partition_all_reduce(worst_all[:, :], worst[:, :], P, bass.bass_isa.ReduceOp.max)\
                .then_inc(worst_reduced, 1)
            pool.wait_ge(verdict_ready, 1)
            one = pool.value_load(onehot[0:1, 0:1], min_val=0, max_val=1)
            with pool.If(one == 1):
                pool.wait_ge(feats_stored, 16 * SB)
                for b in range(BLOCKS):
                    pool.indirect_dma_start(attended[:, b, :], None, feats_dram[:, :],
                                            bass.IndirectOffsetOnAxis(neighbour_u[:, b:b + 1], 0))\
                        .then_inc(gathered[b // BPS], 16)
            pool.wait_ge(verdict_ready, 1)

        @block.tensor
        def _(pe):
            def turn(stream, v, pos):
                q, j = quarters(stream)[pos // BPS], pos % BPS
                n = step_no(stream, v, pos)
                if j == 0:
                    pe.wait_ge(chunk_loaded[q], loaded(stream, v))
                pe.wait_ge(evacuated, n + 1)
                buf = pe_turn[pos % TURN_BUFS]
                for t in range(BPS):
                    ins = pe.transpose(buf[:, t // 4, t % 4 * P:(t % 4 + 1) * P],
                                       ring[:, q, t, j * P:(j + 1) * P], ident[:, :])
                ins.then_inc(turned, 1)

            def multiply(stream, v, pos, rows, ready):
                q = quarters(stream)[pos // BPS]
                n = step_no(stream, v, pos)
                pe.wait_ge(evacuated, n + 1 + TURN_BUFS)
                if pos == 0:
                    pe.wait_ge(sums_copied, SB * TURNED[stream] + v)
                if pos % BPS == 0 and isinstance(v, int) and ready is not None:
                    sem_, first = ready
                    pe.wait_ge(sem_, first + pos // BPS + 1)
                for half in range(2):
                    ins = pe.matmul(pe_sum[F * half:F * half + F, :], rows[:, BPS * q + pos % BPS, :],
                                    tiles[:, pos % TILE_BUFS, half * HALF:(half + 1) * HALF],
                                    start=(pos == 0), stop=(pos == STEPS - 1))
                ins.then_inc(multiplied, 1)

            def project(bank, paired_terms, count):
                filled, read = (rows_filled, rows_read) if bank is pe_rows else (flip_filled, flip_read)
                pe.wait_ge(read, count)
                for t in range(BPS // 2):
                    for i, (source, w) in enumerate(paired_terms):
                        ins = pe.matmul(pairs(t)(bank), source[:, t * P:(t + 1) * P],
                                        wb[:, w, :].rearrange("p (h f) -> p h f", h=2),
                                        start=(i == 0), stop=(i == len(paired_terms) - 1))
                ins.then_inc(filled, 1)

            def flip(turn_no, count):
                pe.wait_ge(staged, turn_no + 1)
                pe.wait_ge(flip_read, count)
                for t in range(BPS // 2):
                    pair = [a[:, 2 * t:2 * t + 2, :].rearrange("p b f -> p (b f)") for a in (pe_flip, staged_rows)]
                    ins = pe.transpose(pair[0], pair[1], ident[:, :])
                ins.then_inc(flip_filled, 1)

            def visit(stream, v, rows, ready, finish, extra):
                first = isinstance(v, int)
                turn(stream, v, 0)
                if not first:
                    finish(v - 1)
                for pos in range(1, STEPS):
                    turn(stream, v, pos)
                    multiply(stream, v, pos - 1, rows, ready)
                    for at, needs_before, act in extra:
                        if at == pos and not (first and needs_before):
                            act(v)
                multiply(stream, v, STEPS - 1, rows, ready)

            def product(stream, rows, ready, finish, extra=()):
                visit(stream, 0, rows, ready, finish, extra)
                with pe.Fori(1, SB) as v:
                    visit(stream, v, rows, ready, finish, extra)
                finish(SB - 1)

            def sums_ready(stream, v):
                pe.wait_ge(sums_copied, SB * TURNED[stream] + v + 1)

            pe.wait_ge(consts_ready, 2)

            def finish_hop1(v):
                sums_ready(HOP1, v)
                pe.wait_ge(flip_read, flip_hop1(v) + 1)
                project(pe_rows, [(sums, W_H1A), (paired, W_H1X)], rows_hop1(v))

            pe.wait_ge(x_loaded, 16)
            pe.wait_ge(small_loaded, 16 * 12)
            product(HOP1, x0, None, finish_hop1, [(8, False, lambda v: flip(v, flip_hop1(v)))])

            def finish_hop2(v):
                sums_ready(HOP2, v)
                pe.wait_ge(flip_read, flip_hop2(v) + 1)
                project(pe_rows, [(sums, W_H2A), (paired, W_H2X)], rows_hop2(v))

            def gcn_flip(v):
                flip(5 + 2 * v, flip_gcn(v))

            def gcn_rows(v):
                pe.wait_ge(flip_read, flip_gcn(v) + 1)
                project(pe_rows, [(paired, W_GCN)], rows_gcn(v))

            product(HOP2, hop, (rows_read, rows_hop1(0)), finish_hop2,
                    [(8, True, lambda v: gcn_flip(v - 1)), (16, True, lambda v: gcn_rows(v - 1)),
                     (24, False, lambda v: flip(4 + 2 * v, flip_hop2(v)))])
            gcn_flip(SB - 1)
            gcn_rows(SB - 1)

            pe.wait_ge(rows_read, rows_spread(0))
            pe.wait_ge(evacuated, step_no(CHEB1, 0, 0) + TURN_BUFS)
            for v in range(SB):
                s = superblock(SPREAD, v)
                for q in quarters(SPREAD):
                    pe.wait_ge(chunk_loaded[q], loaded(SPREAD, v))
                    for t in range(BPS):
                        for half in range(2):
                            ins = pe.matmul(pe_turn[q // 2][F * half:F * half + F, q % 2, :],
                                            z[:, BPS * s + t, :], ring[:, q, t, half * HALF:(half + 1) * HALF],
                                            start=(v == 0 and t == 0), stop=(v == SB - 1 and t == BPS - 1),
                                            skip_group_check=True)
                    ins.then_inc(spread, 1)

            def spread_rows(q):
                pe.wait_ge(spread_copied, q + 1)
                project(pe_rows, [(spread_sums[:, q, :], W_ONE)], rows_spread(q))

            spread_rows(0)
            pe.wait_ge(spread_copied, SB)

            def finish_cheb1(v):
                sums_ready(CHEB1, v)
                project(pe_rows, [(sums, W_ONE)], rows_cheb1(v))
                pe.wait_ge(flip_read, flip_cheb1(v) + 1)
                project(pe_flip, [(sums, W_C1), (paired, W_C0)], filt_cheb1(v))

            product(CHEB1, y2, (y2_ready, 0), finish_cheb1,
                    [(24, False, lambda v: flip(12 + v, flip_cheb1(v)))]
                    + [(1 + 8 * (q - 1), False, lambda v, q=q: spread_rows(q) if isinstance(v, int) else None)
                       for q in range(1, SB)])

            def finish_cheb2(v):
                sums_ready(CHEB2, v)
                project(pe_rows, [(sums, W_ONE)], rows_cheb2(v))
                project(pe_flip, [(sums, W_C2)], filt_cheb2(v))

            product(CHEB2, t1, (rows_read, rows_cheb1(0)), finish_cheb2)

            def finish_cheb3(v):
                sums_ready(CHEB3, v)
                project(pe_flip, [(sums, W_C3)], filt_cheb3(v))

            def gat_flip(v):
                flip(16 + v, flip_gat(v))

            def gat_rows(v):
                pe.wait_ge(flip_read, flip_gat(v) + 1)
                project(pe_rows, [(paired, W_GAT)], rows_gat(v))

            product(CHEB3, t2, (rows_read, rows_cheb2(0)), finish_cheb3,
                    [(10, True, lambda v: gat_flip(v - 1)), (18, True, lambda v: gat_rows(v - 1))])
            gat_flip(SB - 1)
            gat_rows(SB - 1)

            pe.wait_ge(verdict_ready, 1)
            one = pe.value_load(onehot[0:1, 0:1], min_val=0, max_val=1)
            with pe.If(one == 0):
                for c in range(2):
                    ins = pe.transpose(pe_turn[0][:, 0, c * P:(c + 1) * P],
                                       att[:, 1, c * 16:(c + 1) * 16, :].rearrange("p b h -> p (b h)"), ident[:, :])
                ins.then_inc(neigh_turned, 1)
                pe.wait_ge(neigh_copied, 1)
                for g in range(2):
                    with pe.Fori(0, BLOCKS) as b:
                        pe.wait_ge(heads_read, b + (g * BLOCKS + 1))
                        for h in range(4):
                            first = 4 * BLOCKS * g + h
                            pe.wait_ge(probs_ready, b * 4 + (first + 2))
                            for c in range(9):
                                if c < 8:
                                    if c >= 2:
                                        pe.wait_ge(probs_copied, b * 32 + (8 * first + c))
                                    else:
                                        pe.wait_ge(probs_copied, b * 32 + (8 * first + 1))
                                    for t in range(4):
                                        ins = pe.transpose(pe_turn[c % 2][:, 0, t * P:(t + 1) * P],
                                                           probs()[:, (4 * c + t) * P:(4 * c + t + 1) * P], ident[:, :])
                                    ins.then_inc(probs_turned, 1)
                                if c >= 1:
                                    pe.wait_ge(probs_copied, b * 32 + (8 * first + c + 1))
                                    for t in range(4):
                                        j = 4 * (c - 1) + t
                                        head = (4 * g + h) * D
                                        ins = pe.matmul(pe_sum[:, h * D:(h + 1) * D],
                                                        tiles[:, (c - 1) % TILE_BUFS, t * P:(t + 1) * P],
                                                        feats[:, j, head:head + D],
                                                        start=(j == 0), stop=(j == BLOCKS - 1))
                            ins.then_inc(heads_summed, 1)
            pe.wait_ge(verdict_ready, 1)

        @block.scalar
        def _(act):
            act.wait_ge(consts_zeroed, 2)
            for source, w, k in wb_loads:
                for half in range(2):
                    act.dma_start(wb[F * half:F * half + F, w:w + k, F * half:F * half + F], source)\
                        .then_inc(small_loaded, 16)
            for i, source in enumerate(rows_loads):
                act.dma_start(per_row[:, i, :], source.partition_broadcast(P)).then_inc(small_loaded, 16)

            def visit(stream, v, finish):
                for pos in range(STEPS):
                    n = step_no(stream, v, pos)
                    act.wait_ge(turned, n + 1)
                    act.wait_ge(multiplied, n + 1)
                    source = pe_turn[pos % TURN_BUFS][:, :, :].rearrange("p a n -> p (a n)")
                    if stream == HOP1:
                        if pos == 0:
                            act.wait_ge(deg_added, v)
                        act.activation(tiles[:, pos % TILE_BUFS, :], source, ACT.Copy,
                                       accum_out=deg_part[:, pos:pos + 1]).then_inc(evacuated, 1)
                    else:
                        act.activation(tiles[:, pos % TILE_BUFS, :], source, ACT.Copy).then_inc(evacuated, 1)
                    if pos == 0 and not isinstance(v, int):
                        finish(v - 1)
                act.wait_ge(multiplied, step_no(stream, v, STEPS - 1) + 1 + TILE_BUFS)
                act.activation(sums[:, :], pe_sum[:, :], ACT.Copy).then_inc(sums_copied, 1)

            def product(stream, finish):
                visit(stream, 0, finish)
                with act.Fori(1, SB) as v:
                    visit(stream, v, finish)
                finish(SB - 1)

            def finish_hop1(v):
                act.wait_ge(rows_filled, rows_hop1(v) + 1)
                act.activation(rows_of(hop, superblock(HOP1, v)), pe_rows[:, :, :], ACT.Tanh).then_inc(rows_read, 1)

            def finish_hop2(v):
                act.wait_ge(rows_filled, rows_hop2(v) + 1)
                act.activation(second_hop[:, :, :], pe_rows[:, :, :], ACT.Tanh).then_inc(rows_read, 1)

            def finish_cheb1(v):
                act.wait_ge(rows_filled, rows_cheb1(v) + 1)
                act.activation(rows_of(t1, superblock(CHEB1, v)), pe_rows[:, :, :], ACT.Copy).then_inc(rows_read, 1)

            product(HOP1, finish_hop1)
            product(HOP2, finish_hop2)
            act.wait_ge(spread, SB * SB)
            for q in range(SB):
                act.activation(spread_sums[:, q, :], pe_turn[q // 2][:, q % 2, :], ACT.Copy).then_inc(spread_copied, 1)
            product(CHEB1, finish_cheb1)
            product(CHEB2, lambda v: None)
            product(CHEB3, lambda v: None)

            act.wait_ge(verdict_ready, 1)
            one = act.value_load(onehot[0:1, 0:1], min_val=0, max_val=1)
            with act.If(one == 0):
                for g in range(2):
                    with act.Fori(0, BLOCKS) as b:
                        for h in range(4):
                            first = 4 * BLOCKS * g + h
                            act.wait_ge(scores_ready, b * 4 + first + 1)
                            act.wait_ge(probs_turned, b * 32 + (8 * first + 1))
                            act.activation(probs(), scores(), ACT.Exp, bias=neg_max[:, h:h + 1],
                                           accum_out=weight_sum[:, h:h + 1]).then_inc(probs_ready, 1)
                            for c in range(8):
                                act.wait_ge(probs_turned, b * 32 + (8 * first + c + 2))
                                act.activation(tiles[:, c % TILE_BUFS, 0:HALF], pe_turn[c % 2][:, 0, :], ACT.Copy)\
                                    .then_inc(probs_copied, 1)
            act.wait_ge(verdict_ready, 1)

        @block.vector
        def _(dve):
            links = {"before": 0, "here": 0}
            loop = []

            def mark(ins):
                ins.then_inc(vec, 1)
                links["here"] += 1

            def join(apart=False):
                count = links["before"] + links["here"]
                if loop:
                    var, start, per = loop[0]
                    count = var * per + (count - start * per)
                if apart:
                    wait_apart(dve, vec, count, consts_zeroed)
                else:
                    dve.wait_ge(vec, count)

            def link(ins):
                mark(ins)
                join()

            def enter(var, start, per):
                links["before"] += links["here"]
                links["here"] = 0
                loop.append((var, start, per))

            def leave(turns):
                per = loop.pop()[2]
                assert links["here"] == per, f"a turn of the loop has {links['here']} links, not {per}"
                links["before"] += per * turns
                links["here"] = 0

            def inverse_root(y, v_in, t):
                link(dve.tensor_scalar(t.bitcast(U32), v_in.bitcast(U32), 1, None, ALU.logical_shift_right))
                link(dve.tensor_scalar(y.bitcast(I32), t.bitcast(I32), -1.0, float(0x5F3759DF), ALU.mult, ALU.add))
                for _ in range(4):
                    link(dve.tensor_tensor(t, y, y, ALU.mult))
                    link(dve.tensor_tensor(t, t, v_in, ALU.mult))
                    link(dve.tensor_scalar(t, t, -0.5, 1.5, ALU.mult, ALU.add))
                    link(dve.tensor_tensor(y, y, t, ALU.mult))

            def wide(a):
                return a.unsqueeze(2).to_broadcast([P, BPS, F])

            def for_all(i):
                return per_row[:, i, :].unsqueeze(1).to_broadcast([P, BPS, F])

            def norm(final):
                link(dve.tensor_reduce(rowsum[:, :], work[:, :, :], X, ALU.add))
                link(dve.tensor_scalar(rowsum[:, :], rowsum[:, :], -1.0 / F, None, ALU.mult))
                link(dve.tensor_tensor(work[:, :, :], work[:, :, :], wide(rowsum[:, :]), ALU.add))
                link(dve.tensor_tensor(square[:, :, :], work[:, :, :], work[:, :, :], ALU.mult))
                link(dve.tensor_reduce(rowsum[:, :], square[:, :, :], X, ALU.add))
                v = root_x[:, 0:BPS]
                link(dve.tensor_scalar(v, rowsum[:, :], 1.0 / F, EPS, ALU.mult, ALU.add))
                inverse_root(root_y[:, 0:BPS], v, root_t[:, 0:BPS])
                final(work[:, :, :], wide(root_y[:, 0:BPS]))

            def scan(stream, v, r):
                q = quarters(stream)[r]
                base = SCAN * stream
                s = superblock(stream, v)
                wait_apart(dve, chunk_loaded[q], loaded(stream, v), consts_zeroed)
                for t in range(SCAN):
                    ins = dve.max(top8[:, t, :], ring[:, q, base + t, :])
                mark(ins)
                join(apart=True)
                for t in range(SCAN):
                    ins = dve.max_index(top8_at[:, t, :], top8[:, t, :], ring[:, q, base + t, :])
                ins.then_inc(scanned, 1)
                wait_apart(dve, scanned, SB * SB * stream + SB * v + r + 1, consts_zeroed)
                mark(dve.tensor_copy(top2[:, bass.ds(s * BPS + base, SCAN), q, :], top8[:, :, 0:2]))
                mark(dve.tensor_copy(top_at[:, bass.ds(s * BPS + base, SCAN), q], top8_at[:, :, 0]))
                join(apart=True)

            def stage(buf, s):
                dve.tensor_copy(staged_by_half(), split(rows_of(buf, s))).then_inc(staged, 1)

            def take_flip(count):
                dve.wait_ge(flip_filled, count + 1)
                source = pe_flip[:, :, :].rearrange("p b f -> p (b f)")
                dve.tensor_copy(paired[:, :], source).then_inc(flip_read, 1)

            def visits(body, per):
                body(0)
                with dve.Fori(1, SB) as v:
                    enter(v, 1, per)
                    body(v)
                    leave(SB - 1)

            dve.wait_ge(small_loaded, 16 * 12)
            dve.wait_ge(consts_zeroed, 3)
            dve.wait_ge(x_loaded, 16)
            mark(dve.tensor_tensor(wb[:, W_C0, :], wb[:, W_C0, :], wb[:, W_C2, :], ALU.subtract))
            link(dve.tensor_tensor(wb[:, W_C1, :], wb[:, W_C1, :], wb[:, W_C3, :], ALU.subtract))
            link(dve.tensor_scalar(wb[:, W_C2:W_C3 + 1, :], wb[:, W_C2:W_C3 + 1, :], 2.0, None, ALU.mult))

            def hop1(v):
                stage(x0, superblock(HOP1, v))
                scan(HOP1, v, 0)
                take_flip(flip_hop1(v))
                for r in range(1, SB):
                    scan(HOP1, v, r)
                dve.wait_ge(evacuated, step_no(HOP1, v, STEPS - 1) + 1 + TURN_BUFS)
                dve.tensor_tensor(deg[:, :], deg[:, :], deg_part[:, :], ALU.add).then_inc(deg_added, 1)
                dve.wait_ge(deg_added, v + 1)

            visits(hop1, 12)

            link(dve.tensor_scalar(root_x[:, :], deg[:, :], 1e-30, None, ALU.max))
            inverse_root(root_y[:, :], root_x[:, :], root_t[:, :])
            link(dve.tensor_scalar(root_t[:, :], deg[:, :], 0.0, None, ALU.is_gt))
            link(dve.tensor_tensor(dinv[:, :], root_y[:, :], root_t[:, :], ALU.mult))

            def norm_hop2(v):
                s = superblock(HOP2, v)
                wait_apart(dve, rows_read, rows_hop2(v) + 1, consts_zeroed)
                link(dve.tensor_tensor(work[:, :, :], second_hop[:, :, :], rows_of(x0, s), ALU.add))
                norm(lambda rows, factor: dve.tensor_tensor(staged_by_half(), split(rows), split(factor), ALU.mult)
                     .then_inc(staged, 1))
                dve.wait_ge(staged, 6 + 2 * v)
                link(dve.tensor_copy(split(rows_of(y1, s)), staged_by_half()))

            def scale_z(v):
                s = superblock(HOP2, v)
                wait_apart(dve, rows_filled, rows_gcn(v) + 1, consts_zeroed)
                factor = dinv[:, bass.ds(s * BPS, BPS)].unsqueeze(2).to_broadcast([P, BPS, F])
                dve.tensor_tensor(rows_of(z, s), pe_rows[:, :, :], factor, ALU.mult).then_inc(rows_read, 1)

            def hop2(v):
                first = isinstance(v, int)
                if not first:
                    norm_hop2(v - 1)
                scan(HOP2, v, 0)
                if not first:
                    take_flip(flip_gcn(v - 1))
                scan(HOP2, v, 1)
                if not first:
                    scale_z(v - 1)
                stage(hop, superblock(HOP2, v))
                scan(HOP2, v, 2)
                take_flip(flip_hop2(v))
                scan(HOP2, v, 3)

            dve.wait_ge(rows_read, rows_hop1(SB - 1) + 1)
            visits(hop2, 38)
            norm_hop2(SB - 1)
            take_flip(flip_gcn(SB - 1))
            scale_z(SB - 1)

            for b in range(BLOCKS):
                ins = dve.max(best[:, b, :], top2[:, b, :, :].rearrange("p q k -> p (q k)"))
            link(ins)
            largest = best[:, :, 0:1].to_broadcast([P, BLOCKS, SB])
            for q in range(SB):
                mark(dve.tensor_scalar(top_at[:, :, q], top_at[:, :, q], float(q * QUARTER), None, ALU.add))
            link(dve.tensor_tensor(hit[:, :, :], top2[:, :, :, 0], largest, ALU.is_equal))
            link(dve.tensor_tensor(hit[:, :, :], hit[:, :, :], top_at[:, :, :], ALU.mult))
            link(dve.tensor_reduce(neighbour[:, :], hit[:, :, :], X, ALU.add))
            link(dve.tensor_copy(neighbour_u[:, :], neighbour[:, :]))
            for k in range(2):
                link(dve.tensor_scalar(lead[:, k, :], best[:, :, k], -1.0, 1.0, ALU.mult, ALU.add))
                link(dve.tensor_scalar(lead[:, k, :], lead[:, k, :], NEG, None, ALU.mult))
            link(dve.tensor_tensor(lead[:, 1, :], lead[:, 1, :], lead[:, 0, :], ALU.subtract))
            link(dve.tensor_scalar(lead[:, 2, :], lead[:, 0, :], 2.0 ** -20, None, ALU.mult))
            link(dve.scalar_tensor_tensor(lead[:, 2, :], lead[:, 2, :], -1.0, lead[:, 2, :], ALU.mult, ALU.max))
            link(dve.scalar_tensor_tensor(lead[:, 2, :], lead[:, 1, :], 0.99, lead[:, 2, :], ALU.mult, ALU.add))
            link(dve.tensor_reduce(worst[:, 0:1], lead[:, 2, :], X, ALU.max))

            for q in range(SB):
                blocks = slice(q * BPS, (q + 1) * BPS)
                dve.wait_ge(rows_filled, rows_spread(q) + 1)
                dve.tensor_tensor(work[:, :, :], pe_rows[:, :, :], z[:, blocks, :], ALU.add).then_inc(rows_read, 1)
                dve.wait_ge(rows_read, rows_spread(q) + 1)
                link(dve.tensor_tensor(work[:, :, :], work[:, :, :], wide(dinv[:, blocks]), ALU.mult))
                link(dve.tensor_tensor(work[:, :, :], work[:, :, :], for_all(0), ALU.add))
                link(dve.scalar_tensor_tensor(work[:, :, :], work[:, :, :], 0.0, y1[:, blocks, :], ALU.max, ALU.add))
                norm(lambda rows, factor: dve.tensor_tensor(y2[:, blocks, :], rows, factor, ALU.mult)
                     .then_inc(y2_ready, 1))
            dve.wait_ge(y2_ready, SB)

            def keep_cheb1(v):
                wait_apart(dve, flip_filled, filt_cheb1(v) + 1, consts_zeroed)
                dve.tensor_copy(rows_of(filtered, superblock(CHEB1, v)), pe_flip[:, :, :]).then_inc(flip_read, 1)

            def cheb1(v):
                if not isinstance(v, int):
                    keep_cheb1(v - 1)
                stage(y2, superblock(CHEB1, v))
                take_flip(flip_cheb1(v))

            visits(cheb1, 0)
            keep_cheb1(SB - 1)
            dve.wait_ge(flip_read, filt_cheb1(SB - 1) + 1)

            def keep_cheb2(v):
                s = superblock(CHEB2, v)
                wait_apart(dve, rows_filled, rows_cheb2(v) + 1, consts_zeroed)
                dve.scalar_tensor_tensor(rows_of(t2, s), pe_rows[:, :, :], 2.0, rows_of(y2, s),
                                         ALU.mult, ALU.subtract).then_inc(rows_read, 1)
                wait_apart(dve, flip_filled, filt_cheb2(v) + 1, consts_zeroed)
                dve.tensor_tensor(rows_of(filtered, s), rows_of(filtered, s), pe_flip[:, :, :], ALU.add)\
                    .then_inc(flip_read, 1)

            with dve.Fori(0, SB) as v:
                keep_cheb2(v)
            dve.wait_ge(flip_read, filt_cheb2(SB - 1) + 1)

            def norm_cheb3(v):
                s = superblock(CHEB3, v)
                wait_apart(dve, flip_filled, filt_cheb3(v) + 1, consts_zeroed)
                dve.tensor_tensor(work[:, :, :], rows_of(filtered, s), pe_flip[:, :, :], ALU.add).then_inc(flip_read, 1)
                dve.wait_ge(flip_read, filt_cheb3(v) + 1)
                link(dve.tensor_tensor(work[:, :, :], work[:, :, :], rows_of(y2, s), ALU.add))
                norm(lambda rows, factor: dve.tensor_tensor(staged_by_half(), split(rows), split(factor), ALU.mult)
                     .then_inc(staged, 1))
                dve.wait_ge(staged, 17 + v)
                link(dve.tensor_copy(split(rows_of(y3, s)), staged_by_half()))
                take_flip(flip_gat(v))
                wait_apart(dve, rows_filled, rows_gat(v) + 1, consts_zeroed)
                dve.tensor_copy(rows_of(feats, s), pe_rows[:, :, :]).then_inc(rows_read, 1)
                dve.wait_ge(rows_read, rows_gat(v) + 1)
                for i in range(2):
                    link(dve.tensor_tensor(square[:, :, :], rows_of(feats, s), for_all(1 + i), ALU.mult))
                    link(dve.tensor_reduce(att[:, i, bass.ds(s * BPS, BPS), :],
                                           square[:, :, :].rearrange("p b (h d) -> p b h d", h=H), X, ALU.add))

            with dve.Fori(0, SB) as v:
                enter(v, 0, 30)
                norm_cheb3(v)
                leave(SB)

            for i in range(2):
                att_i = att[:, i, :, :].rearrange("p b h -> p (b h)")
                ins = dve.tensor_reduce(worst[:, 1 + i:2 + i], att_i, X, ALU.max, apply_absolute_value=True)
            ins.then_inc(worst_found, 1)
            dve.wait_ge(worst_reduced, 1)
            link(dve.tensor_tensor(verdict[:, 0:1], worst_all[:, 1:2], worst_all[:, 2:3], ALU.add))
            link(dve.tensor_scalar(verdict[:, 0:1], verdict[:, 0:1], 2.0, 128.0, ALU.mult, ALU.add))
            link(dve.tensor_tensor(verdict[:, 1:2], verdict[:, 0:1], worst_all[:, 0:1], ALU.add))
            dve.tensor_scalar(onehot[:, :], verdict[:, 1:2], 0.0, None, ALU.is_lt).then_inc(verdict_ready, 1)
            dve.wait_ge(verdict_ready, 1)
            one = dve.value_load(onehot[0:1, 0:1], min_val=0, max_val=1)

            def last_norm(s):
                blocks = slice(s * BPS, (s + 1) * BPS)
                dve.wait_ge(out_ready, s)
                link(dve.tensor_tensor(work[:, :, :], attended[:, blocks, :], for_all(3), ALU.add))
                link(dve.scalar_tensor_tensor(work[:, :, :], work[:, :, :], 0.0, y3[:, blocks, :], ALU.max, ALU.add))
                norm(lambda rows, factor: dve.tensor_tensor(attended[:, blocks, :], rows, factor, ALU.mult)
                     .then_inc(out_ready, 1))

            taken = links["before"] + links["here"]
            with dve.If(one == 1):
                for s in range(SB):
                    dve.wait_ge(gathered[s], 16 * BPS)
                    last_norm(s)
            links.update(before=taken, here=0)
            with dve.Else():
                dve.wait_ge(neigh_turned, 1)
                dve.tensor_copy(staged_rows[:, :, :].rearrange("p b f -> p (b f)")[:, 0:2 * P],
                                pe_turn[0][:, 0, 0:2 * P]).then_inc(neigh_copied, 1)
                for g in range(2):
                    dve.wait_ge(neigh_loaded, 64 * (g + 1))
                    with dve.Fori(0, BLOCKS) as b:
                        enter(b, 0, 19)
                        dve.wait_ge(mask_loaded, b * 16 + (g * BLOCKS + 1) * 16)
                        link(dve.tensor_scalar(mask(), mask(), -1.0, 1.0, ALU.mult, ALU.add))
                        link(dve.tensor_scalar(mask(), mask(), NEG, None, ALU.mult))
                        for h in range(4):
                            head = 4 * g + h
                            first = 4 * BLOCKS * g + h
                            dve.wait_ge(probs_ready, b * 4 + (first + 1))
                            link(dve.tensor_scalar(scores(), neigh_terms(h), att[:, 0, bass.ds(b, 1), head],
                                                   None, ALU.add))
                            link(dve.scalar_tensor_tensor(scores(), scores(), 0.2, scores(), ALU.mult, ALU.max))
                            link(dve.tensor_tensor(scores(), scores(), mask(), ALU.add))
                            link(dve.tensor_reduce(neg_max[:, h:h + 1], scores(), X, ALU.max))
                            dve.tensor_scalar(neg_max[:, h:h + 1], neg_max[:, h:h + 1], -1.0, None, ALU.mult)\
                                .then_inc(scores_ready, 1)
                        dve.wait_ge(heads_summed, b * 4 + (4 * BLOCKS * g + 4))
                        link(dve.reciprocal(weight_sum[:, :], weight_sum[:, :]))
                        dst = attended[:, bass.ds(b, 1), 4 * g * D:4 * (g + 1) * D].rearrange("p b (h d) -> p (b h) d", h=4)
                        dve.tensor_tensor(dst, pe_sum[:, 0:4 * D].rearrange("p (h d) -> p h d", h=4),
                                                 weight_sum[:, :].unsqueeze(2).to_broadcast([P, 4, D]), ALU.mult)\
                            .then_inc(heads_read, 1)
                        leave(BLOCKS)
                dve.wait_ge(heads_read, 2 * BLOCKS + 1)
                for s in range(SB):
                    last_norm(s)
            dve.wait_ge(verdict_ready, 1)


_INS = ['x', 'adj', 'L0_gnn_W', 'L1_gnn_W', 'L1_gnn_b', 'L2_gnn_weight', 'L3_gnn_W',
        'L3_gnn_att_self', 'L3_gnn_att_neigh', 'L3_gnn_bias']
_OUTS = [((4096, 64), 'float32')]


def kernel(**inputs):
    import numpy as _np
    import concourse.bacc as _bacc
    from concourse import mybir as _mybir
    from concourse.bass_utils import run_bass_kernel_spmd as _run

    nc = _bacc.Bacc("TRN2", target_bir_lowering=False, num_devices=1)
    arrays, args = {}, []
    for name in _INS:
        a = _np.ascontiguousarray(inputs[name])
        arrays[f"in_{name}_dram"] = a
        args.append(nc.dram_tensor(f"in_{name}_dram", a.shape, _mybir.dt.from_np(a.dtype), kind="ExternalInput").ap())
    for i, (shape, dtype) in enumerate(_OUTS):
        dt = _mybir.dt.from_np(_np.dtype(dtype))
        args.append(nc.dram_tensor(f"out_{i}_dram", shape, dt, kind="ExternalOutput").ap())
    build(nc, *args)
    r = _run(nc, [arrays], core_ids=[0])
    return r.results[0]["out_0_dram"]
```

```python
from contextlib import ExitStack

import concourse.bass as bass
from concourse import mybir

F32 = mybir.dt.float32
U32 = mybir.dt.uint32
I32 = mybir.dt.int32
ALU = mybir.AluOpType
ACT = mybir.ActivationFunctionType
X = mybir.AxisListType.X

P = 128
N, F = 4096, 64
H, D = 8, 8
BLOCKS = N // P
SB = 4
BPS = BLOCKS // SB
QUARTER = N // SB
HALF = QUARTER // 2
STEPS = BLOCKS
TURN_BUFS, TILE_BUFS = 2, 4
SCAN = 4
RUN = QUARTER // 4
NATURAL = SB - 1
OTHERS = (SB - 1) * BPS
PIECES = 4
EPS = 1e-5
NEG = -1e10

HOP1, HOP2, SPREAD, CHEB1, CHEB2, CHEB3 = range(6)
TURNED = {HOP1: 0, HOP2: 1, CHEB1: 2, CHEB2: 3, CHEB3: 4}

W_H1A, W_H1X, W_H2A, W_H2X, W_GCN, W_C0, W_C1, W_C2, W_C3, W_GAT, W_ONE = range(11)


def superblock(stream, v):
    return v if stream % 2 == 0 else SB - 1 - v


def quarters(stream):
    return [3, 2, 1, 0] if stream == CHEB2 else [0, 1, 2, 3]


def loaded(stream, v, q):
    if q == NATURAL:
        first = 1 + (SB - 1) * stream
    else:
        first = (1, 4, 8, 12, 15, 18)[stream]
    return 16 * PIECES * (first + v)


def step_no(stream, v, pos):
    return STEPS * SB * TURNED[stream] + STEPS * v + pos


def by_pe(stream, pos):
    return quarters(stream)[pos // BPS] == NATURAL


def pe_no(stream, v, pos):
    return BPS * SB * TURNED[stream] + BPS * v + pos % BPS


def dve_no(stream, v, pos):
    return OTHERS * SB * TURNED[stream] + OTHERS * v + (pos - BPS if by_pe(stream, 0) else pos)


def scan_no(stream, v, q, half):
    return 2 * v + half if stream == HOP1 else 2 * SB + 2 * (SB - 1) * v + 2 * q + half


def rows_hop1(v):
    return 1 + v


def rows_hop2(v):
    return 5 + 2 * v


def rows_gcn(v):
    return 6 + 2 * v


def rows_spread(q):
    return 13 + q


def rows_cheb1(v):
    return 17 + v


def rows_cheb2(v):
    return 21 + v


def rows_gat(v):
    return 25 + v


def flip_hop1(v):
    return 1 + v


def flip_hop2(v):
    return 5 + 2 * v


def flip_gcn(v):
    return 6 + 2 * v


def flip_cheb1(v):
    return 13 + 2 * v


def filt_cheb1(v):
    return 14 + 2 * v


def filt_cheb2(v):
    return 21 + v


def filt_cheb3(v):
    return 25 + 2 * v


def flip_gat(v):
    return 26 + 2 * v


def wait_apart(eng, semaphore, value, holds):
    if isinstance(value, int):
        eng.wait_ge(semaphore, value)
        return
    value = eng.to_reg(value)
    eng.wait_ge(holds, 1)
    eng.wait_ge(semaphore, value)


def build(nc, x, adj, w_hop, w_gcn, b_gcn, w_cheb, w_gat, att_self, att_neigh, b_gat, out):
    ctx = ExitStack()
    with ctx:
        def sb(name, shape, dt=F32):
            return ctx.enter_context(nc.sbuf_tensor(name, shape, dt))

        def ps(name, shape):
            return ctx.enter_context(nc.psum_tensor(name, shape, F32))

        def sem(name):
            return ctx.enter_context(nc.semaphore(name))

        feats_dram = nc.dram_tensor("feats_scratch", [N, F], F32, kind="Internal")
        att_dram = nc.dram_tensor("att_scratch", [2, N, H], F32, kind="Internal")
        neigh_dram = nc.dram_tensor("neigh_scratch", [BLOCKS * H, P], F32, kind="Internal")

        ring = sb("ring", [P, SB, BPS, QUARTER])
        tiles = sb("tiles", [P, TILE_BUFS, QUARTER])
        buf_a = sb("buf_a", [P, BLOCKS, F])
        buf_b = sb("buf_b", [P, BLOCKS, F])
        buf_c = sb("buf_c", [P, BLOCKS, F])
        buf_d = sb("buf_d", [P, BLOCKS, F])
        x0 = y2 = buf_a
        hop = buf_b
        t2 = attended = buf_b
        y1 = t1 = y3 = buf_c
        z = filtered = feats = buf_d
        spread_sums = buf_b[:, :, :].rearrange("p b f -> p (b f)").rearrange("p (q n) -> p q n", q=SB)

        ident = sb("ident", [P, P])
        wb = sb("wb", [P, 11, P])
        per_row = sb("per_row", [P, 4, F])
        sums = sb("sums", [P, HALF])
        staged_rows = sb("staged_rows", [P, BPS, F])
        paired = sb("paired", [P, HALF])
        second_hop = sb("second_hop", [P, BPS, F])
        spare = sb("spare", [P, 2 * BPS, F])
        work, square = spare[:, 0:BPS, :], spare[:, BPS:2 * BPS, :]
        rowsum = sb("rowsum", [P, BPS])
        root_t = sb("root_t", [P, BLOCKS])
        root_y = sb("root_y", [P, BLOCKS])
        root_x = sb("root_x", [P, BLOCKS])
        deg_part = sb("deg_part", [P, BLOCKS])
        deg = sb("deg", [P, BLOCKS])
        dinv = sb("dinv", [P, BLOCKS])
        top8 = sb("top8", [P, SCAN, 8])
        top8_at = sb("top8_at", [P, SCAN, 8], U32)
        top2 = sb("top2", [P, BLOCKS, SB, 2])
        top_at = sb("top_at", [P, BLOCKS, SB])
        best = sb("best", [P, BLOCKS, 8])
        hit = sb("hit", [P, BLOCKS, SB])
        neighbour = sb("neighbour", [P, BLOCKS])
        neighbour_u = sb("neighbour_u", [P, BLOCKS], U32)
        lead = sb("lead", [P, 3, BLOCKS])
        att = sb("att", [P, 2, BLOCKS, H])
        worst = sb("worst", [P, 3])
        worst_all = sb("worst_all", [P, 3])
        verdict = sb("verdict", [P, 2])
        onehot = sb("onehot", [P, 1], I32)
        neg_max = sb("neg_max", [P, 4])
        weight_sum = sb("weight_sum", [P, 4])

        pe_turn = [ps(f"pe_turn{i}", [P, 2, HALF]) for i in range(TURN_BUFS)]
        pe_sum = ps("pe_sum", [P, HALF])
        pe_rows = ps("pe_rows", [P, BPS, F])
        pe_flip = ps("pe_flip", [P, BPS, F])

        chunk_loaded = [sem(f"chunk_loaded{q}") for q in range(SB)]
        x_loaded = sem("x_loaded")
        small_loaded = sem("small_loaded")
        consts_zeroed = sem("consts_zeroed")
        consts_ready = sem("consts_ready")
        pe_turned = sem("pe_turned")
        evacuated = sem("evacuated")
        dve_turned = sem("dve_turned")
        degrees_taken = sem("degrees_taken")
        multiplied = sem("multiplied")
        sums_copied = sem("sums_copied")
        rows_filled = sem("rows_filled")
        rows_read = sem("rows_read")
        flip_filled = sem("flip_filled")
        flip_read = sem("flip_read")
        staged = sem("staged")
        scanned = sem("scanned")
        deg_added = sem("deg_added")
        spread = sem("spread")
        spread_copied = sem("spread_copied")
        y2_ready = sem("y2_ready")
        vec = sem("vec")
        feats_stored = sem("feats_stored")
        worst_found = sem("worst_found")
        worst_reduced = sem("worst_reduced")
        verdict_ready = sem("verdict_ready")
        gathered = [sem(f"gathered{s}") for s in range(SB)]
        out_ready = sem("out_ready")
        out_stored = sem("out_stored")
        att_stored = sem("att_stored")
        in_order = sem("in_order")
        neigh_turned = sem("neigh_turned")
        neigh_copied = sem("neigh_copied")
        neigh_stored = sem("neigh_stored")
        neigh_loaded = sem("neigh_loaded")
        mask_loaded = sem("mask_loaded")
        scores_ready = sem("scores_ready")
        probs_ready = sem("probs_ready")
        probs_turned = sem("probs_turned")
        probs_copied = sem("probs_copied")
        heads_summed = sem("heads_summed")
        heads_read = sem("heads_read")
        attended_stored = sem("attended_stored")
        attended_back = sem("attended_back")

        x_rows = x.rearrange("(s p m) f -> s p m f", p=P, m=BPS)
        out_rows = out.rearrange("(s p m) f -> s p m f", p=P, m=BPS)
        feats_rows = feats_dram[:, :].rearrange("(s p m) f -> s p m f", p=P, m=BPS)
        ring_flat = ring[:, :, :, :].rearrange("p q t n -> p q (t n)")
        ring_runs = ring_flat.rearrange("p q (k e) -> p q k e", e=RUN)

        def rows_of(buf, s):
            return buf[:, bass.ds(s * BPS, BPS), :]

        def split(a):
            return a.rearrange("p (h t) f -> p h t f", h=2)

        def staged_by_half():
            return staged_rows[:, :, :].rearrange("p (t h) f -> p h t f", h=2)

        def pairs(t):
            return lambda a: a[:, t::BPS // 2, :]

        wb_loads = [(w_hop.rearrange("k (a f) g -> f (k a) g", a=2), W_H1A, 4),
                    (w_gcn.rearrange("f (k g) -> f k g", k=1), W_GCN, 1),
                    (w_cheb.rearrange("k f g -> f k g"), W_C0, 4),
                    (w_gat.rearrange("f (k g) -> f k g", k=1), W_GAT, 1)]
        rows_loads = [b_gcn, att_self.rearrange("h d -> (h d)"), att_neigh.rearrange("h d -> (h d)"),
                      b_gat.rearrange("h d -> (h d)")]

        flat_ring = ring[:, :, :, :].rearrange("p q t n -> p (q t n)")

        def neigh_terms(h):
            return flat_ring[:, h * N:(h + 1) * N]

        def mask():
            return flat_ring[:, 4 * N:5 * N]

        def scores():
            return flat_ring[:, 5 * N:6 * N]

        def probs():
            return flat_ring[:, 6 * N:7 * N]

        block = ctx.enter_context(nc.Block())

        @block.sync
        def _(sp):
            def load(stream, s, q):
                cols = slice(q * QUARTER, (q + 1) * QUARTER)
                for i in range(PIECES):
                    if q == NATURAL or stream == SPREAD:
                        rows = adj[bass.ds(s * QUARTER, QUARTER), cols].rearrange("(p m) j -> p m j", m=BPS)
                        two = slice(i * BPS // PIECES, (i + 1) * BPS // PIECES)
                        ins = sp.dma_start(ring[:, q, two, :], rows[:, two, :])
                    else:
                        rows = adj[bass.ds(s * QUARTER + i * RUN, RUN), cols]
                        ins = sp.dma_start(ring_runs[:, q, i::PIECES, :],
                                           rows.rearrange("(c m) (a e) -> a c m e", m=BPS, e=RUN))
                    ins.then_inc(chunk_loaded[q], 16)

            for s in range(SB):
                sp.dma_start(rows_of(x0, s), x_rows[s]).then_inc(x_loaded, 16)
            for q in range(SB):
                load(HOP1, 0, q)

            def reload(stream, v):
                for r, q in enumerate(quarters(stream)):
                    if stream != SPREAD and q == NATURAL:
                        wait_apart(sp, pe_turned, pe_no(stream, v - 1, 0) + BPS, consts_zeroed)
                    elif stream != SPREAD:
                        wait_apart(sp, dve_turned, dve_no(stream, v - 1, BPS * r) + BPS, consts_zeroed)
                    else:
                        wait_apart(sp, spread, SB * (v - 1) + r + 1, consts_zeroed)
                    if (stream == HOP1) if q == NATURAL else (stream == SPREAD):
                        wait_apart(sp, scanned, scan_no(stream, v - 1, q, 1) + 1, consts_zeroed)
                    load(stream, superblock(stream, v), q)

            for stream in range(6):
                if stream == HOP2:
                    sp.wait_ge(scanned, 2 * SB)
                if stream == SPREAD:
                    for q in range(NATURAL):
                        sp.wait_ge(dve_turned, dve_no(HOP2, SB - 1, BPS * q) + BPS)
                        load(SPREAD, superblock(SPREAD, 0), q)
                if stream == CHEB1:
                    for q in range(NATURAL):
                        sp.wait_ge(spread, SB * (SB - 1) + q + 1)
                        sp.wait_ge(scanned, scan_no(SPREAD, SB - 1, q, 1) + 1)
                        load(CHEB1, superblock(CHEB1, 0), q)
                with sp.Fori(1, SB) as v:
                    reload(stream, v)
            for v in range(SB):
                s = superblock(CHEB3, v)
                sp.wait_ge(rows_read, rows_gat(v) + 1)
                sp.dma_start(feats_rows[s], rows_of(feats, s)).then_inc(feats_stored, 16)
            sp.wait_ge(feats_stored, 16 * SB)

            sp.wait_ge(verdict_ready, 1)
            one = sp.value_load(onehot[0:1, 0:1], min_val=0, max_val=1)
            with sp.If(one == 0):
                for i in range(2):
                    for s in range(SB):
                        sp.dma_start(att_dram[i].rearrange("(s p m) h -> s p m h", p=P, m=BPS)[s],
                                     att[:, i, s * BPS:(s + 1) * BPS, :]).then_inc(att_stored, 16)
                sp.wait_ge(att_stored, 16 * 2 * SB)
                sp.dma_start(feats[:, :, :], feats_dram[:, :].rearrange("(b p) f -> p b f", p=P)).then_inc(in_order, 16)
                for i in range(2):
                    sp.dma_start(att[:, i, :, :], att_dram[i].rearrange("(b p) h -> p b h", p=P)).then_inc(in_order, 16)
                sp.wait_ge(neigh_copied, 1)
                sp.dma_start(neigh_dram[:, :].rearrange("(c b) p -> b c p", c=2),
                             staged_rows[:, :, :].rearrange("p b f -> p (b f)")[:, 0:2 * P]
                             .rearrange("p (c n) -> p c n", c=2)).then_inc(neigh_stored, 16)
                sp.wait_ge(neigh_stored, 16)
                neigh_all = neigh_dram[:, :].rearrange("(b h) p -> h b p", h=H)
                for g in range(2):
                    sp.wait_ge(heads_read, g * BLOCKS + 1)
                    for h in range(4):
                        sp.dma_start(neigh_terms(h).rearrange("p (b n) -> p b n", b=BLOCKS),
                                     neigh_all[4 * g + h].partition_broadcast(P)).then_inc(neigh_loaded, 16)
                    with sp.Fori(0, BLOCKS) as b:
                        wait_apart(sp, heads_read, b + (g * BLOCKS + 1), consts_zeroed)
                        sp.dma_start(mask(), adj[bass.ds(b * P, P), :]).then_inc(mask_loaded, 16)
                        wait_apart(sp, mask_loaded, b * 16 + (g * BLOCKS + 1) * 16, consts_zeroed)
                sp.wait_ge(heads_read, 2 * BLOCKS + 1)
                sp.dma_start(feats_dram[:, :].rearrange("(b p) f -> p b f", p=P), attended[:, :, :])\
                    .then_inc(attended_stored, 16)
                sp.wait_ge(attended_stored, 16)
                for s in range(SB):
                    sp.dma_start(rows_of(attended, s), feats_rows[s]).then_inc(attended_back, 16)
            for s in range(SB):
                sp.wait_ge(out_ready, s + 1)
                sp.dma_start(out_rows[s], rows_of(attended, s)).then_inc(out_stored, 16)
            sp.wait_ge(out_stored, 16 * SB)

        @block.gpsimd
        def _(pool):
            pool.memset(ident[:, :], 0.0).then_inc(consts_zeroed, 1)
            pool.memset(wb[:, :, :], 0.0).then_inc(consts_zeroed, 1)
            pool.memset(deg[:, :], 1.0).then_inc(consts_zeroed, 1)
            pool.memset(lead[:, 0, :], 0.0).then_inc(evacuated, TURN_BUFS)
            pool.memset(lead[:, 1, :], 0.0).then_inc(multiplied, TILE_BUFS)
            for i, count in enumerate((rows_filled, rows_read, flip_filled, flip_read, heads_read,
                                       probs_ready, probs_turned, probs_copied)):
                pool.memset(lead[:, 2, i:i + 1], 0.0).then_inc(count, 1)
            pool.wait_ge(consts_zeroed, 2)
            pool.affine_select(out=ident[:, :], in_=ident[:, :], compare_op=ALU.not_equal, fill=1.0,
                               base=0, pattern=[[-1, P]], channel_multiplier=1).then_inc(consts_ready, 1)
            pool.affine_select(out=wb[:, W_ONE, :], in_=wb[:, W_ONE, :], compare_op=ALU.not_equal, fill=1.0,
                               base=0, pattern=[[-1, P]], channel_multiplier=1).then_inc(consts_ready, 1)
            pool.wait_ge(worst_found, 1)
            pool.partition_all_reduce(worst_all[:, :], worst[:, :], P, bass.bass_isa.ReduceOp.max)\
                .then_inc(worst_reduced, 1)
            pool.wait_ge(verdict_ready, 1)
            one = pool.value_load(onehot[0:1, 0:1], min_val=0, max_val=1)
            with pool.If(one == 1):
                pool.wait_ge(feats_stored, 16 * SB)
                for b in range(BLOCKS):
                    pool.indirect_dma_start(attended[:, b, :], None, feats_dram[:, :],
                                            bass.IndirectOffsetOnAxis(neighbour_u[:, b:b + 1], 0))\
                        .then_inc(gathered[b // BPS], 16)
            pool.wait_ge(verdict_ready, 1)

        @block.tensor
        def _(pe):
            def turn(stream, v, pos):
                q, j = quarters(stream)[pos // BPS], pos % BPS
                n = pe_no(stream, v, pos)
                if j == 0:
                    pe.wait_ge(chunk_loaded[q], loaded(stream, v, q))
                pe.wait_ge(evacuated, n + 1)
                buf = pe_turn[pos % TURN_BUFS]
                for t in range(BPS):
                    ins = pe.transpose(buf[:, t // 4, t % 4 * P:(t % 4 + 1) * P],
                                       ring[:, q, t, j::BPS], ident[:, :])
                ins.then_inc(pe_turned, 1)

            def multiply(stream, v, pos, rows, ready):
                q = quarters(stream)[pos // BPS]
                if by_pe(stream, pos):
                    pe.wait_ge(evacuated, pe_no(stream, v, pos) + 1 + TURN_BUFS)
                else:
                    pe.wait_ge(dve_turned, dve_no(stream, v, pos) + 1)
                if pos == 0:
                    pe.wait_ge(sums_copied, SB * TURNED[stream] + v)
                if pos % BPS == 0 and isinstance(v, int) and ready is not None:
                    sem_, first = ready
                    pe.wait_ge(sem_, first + pos // BPS + 1)
                for half in range(2):
                    ins = pe.matmul(pe_sum[F * half:F * half + F, :], rows[:, BPS * q + pos % BPS, :],
                                    tiles[:, pos % TILE_BUFS, half * HALF:(half + 1) * HALF],
                                    start=(pos == 0), stop=(pos == STEPS - 1))
                ins.then_inc(multiplied, 1)

            def project(bank, paired_terms, count):
                filled, read = (rows_filled, rows_read) if bank is pe_rows else (flip_filled, flip_read)
                pe.wait_ge(read, count)
                for t in range(BPS // 2):
                    for i, (source, w) in enumerate(paired_terms):
                        ins = pe.matmul(pairs(t)(bank), source[:, t * P:(t + 1) * P],
                                        wb[:, w, :].rearrange("p (h f) -> p h f", h=2),
                                        start=(i == 0), stop=(i == len(paired_terms) - 1))
                ins.then_inc(filled, 1)

            def flip(turn_no, count):
                pe.wait_ge(staged, turn_no + 1)
                pe.wait_ge(flip_read, count)
                for t in range(BPS // 2):
                    pair = [a[:, 2 * t:2 * t + 2, :].rearrange("p b f -> p (b f)") for a in (pe_flip, staged_rows)]
                    ins = pe.transpose(pair[0], pair[1], ident[:, :])
                ins.then_inc(flip_filled, 1)

            def visit(stream, v, rows, ready, finish, extra):
                first = isinstance(v, int)
                for pos in range(STEPS):
                    if by_pe(stream, pos):
                        turn(stream, v, pos)
                    if pos >= 1:
                        multiply(stream, v, pos - 1, rows, ready)
                    if pos == 2 and not first:
                        finish(v - 1)
                    for at, needs_before, act in extra:
                        if at == pos and not (first and needs_before):
                            act(v)
                multiply(stream, v, STEPS - 1, rows, ready)

            def product(stream, rows, ready, finish, extra=()):
                visit(stream, 0, rows, ready, finish, extra)
                with pe.Fori(1, SB) as v:
                    visit(stream, v, rows, ready, finish, extra)
                finish(SB - 1)

            def sums_ready(stream, v):
                pe.wait_ge(sums_copied, SB * TURNED[stream] + v + 1)

            pe.wait_ge(consts_ready, 2)

            def finish_hop1(v):
                sums_ready(HOP1, v)
                pe.wait_ge(flip_read, flip_hop1(v) + 1)
                project(pe_rows, [(sums, W_H1A), (paired, W_H1X)], rows_hop1(v))

            pe.wait_ge(x_loaded, 16 * SB)
            pe.wait_ge(small_loaded, 16 * 12)
            product(HOP1, x0, None, finish_hop1, [(28, False, lambda v: flip(v, flip_hop1(v)))])

            def finish_hop2(v):
                sums_ready(HOP2, v)
                pe.wait_ge(flip_read, flip_hop2(v) + 1)
                project(pe_rows, [(sums, W_H2A), (paired, W_H2X)], rows_hop2(v))

            def gcn_flip(v):
                flip(5 + 2 * v, flip_gcn(v))

            def gcn_rows(v):
                pe.wait_ge(flip_read, flip_gcn(v) + 1)
                project(pe_rows, [(paired, W_GCN)], rows_gcn(v))

            product(HOP2, hop, (rows_read, rows_hop1(0)), finish_hop2,
                    [(29, True, lambda v: gcn_flip(v - 1)), (30, True, lambda v: gcn_rows(v - 1)),
                     (31, False, lambda v: flip(4 + 2 * v, flip_hop2(v)))])
            gcn_flip(SB - 1)
            gcn_rows(SB - 1)

            pe.wait_ge(rows_read, rows_spread(0))
            pe.wait_ge(evacuated, pe_no(CHEB1, 0, 0) + TURN_BUFS)
            for v in range(SB):
                s = superblock(SPREAD, v)
                for q in quarters(SPREAD):
                    pe.wait_ge(chunk_loaded[q], loaded(SPREAD, v, q))
                    for t in range(BPS):
                        columns = ring[:, q, t, :].rearrange("k (p m) -> k m p", m=BPS)
                        for half in range(2):
                            ins = pe.matmul(pe_turn[q // 2][F * half:F * half + F, q % 2, :],
                                            z[:, BPS * s + t, :], columns[:, half * (BPS // 2):(half + 1) * (BPS // 2), :],
                                            start=(v == 0 and t == 0), stop=(v == SB - 1 and t == BPS - 1),
                                            skip_group_check=True)
                    ins.then_inc(spread, 1)

            def spread_rows(q):
                pe.wait_ge(spread_copied, q + 1)
                project(pe_rows, [(spread_sums[:, q, :], W_ONE)], rows_spread(q))

            pe.wait_ge(spread_copied, SB)
            for q in range(SB):
                spread_rows(q)

            def finish_cheb1(v):
                sums_ready(CHEB1, v)
                project(pe_rows, [(sums, W_ONE)], rows_cheb1(v))
                pe.wait_ge(flip_read, flip_cheb1(v) + 1)
                project(pe_flip, [(sums, W_C1), (paired, W_C0)], filt_cheb1(v))

            pe.wait_ge(y2_ready, 1)
            product(CHEB1, y2, None, finish_cheb1, [(28, False, lambda v: flip(12 + v, flip_cheb1(v)))])

            def finish_cheb2(v):
                sums_ready(CHEB2, v)
                project(pe_rows, [(sums, W_ONE)], rows_cheb2(v))
                project(pe_flip, [(sums, W_C2)], filt_cheb2(v))

            product(CHEB2, t1, (rows_read, rows_cheb1(0)), finish_cheb2)

            def finish_cheb3(v):
                sums_ready(CHEB3, v)
                project(pe_flip, [(sums, W_C3)], filt_cheb3(v))

            def gat_flip(v):
                flip(16 + v, flip_gat(v))

            def gat_rows(v):
                pe.wait_ge(flip_read, flip_gat(v) + 1)
                project(pe_rows, [(paired, W_GAT)], rows_gat(v))

            product(CHEB3, t2, (rows_read, rows_cheb2(0)), finish_cheb3,
                    [(29, True, lambda v: gat_flip(v - 1)), (31, True, lambda v: gat_rows(v - 1))])
            gat_flip(SB - 1)
            gat_rows(SB - 1)

            pe.wait_ge(verdict_ready, 1)
            one = pe.value_load(onehot[0:1, 0:1], min_val=0, max_val=1)
            with pe.If(one == 0):
                pe.wait_ge(in_order, 16 * 3)
                for c in range(2):
                    ins = pe.transpose(pe_turn[0][:, 0, c * P:(c + 1) * P],
                                       att[:, 1, c * 16:(c + 1) * 16, :].rearrange("p b h -> p (b h)"), ident[:, :])
                ins.then_inc(neigh_turned, 1)
                pe.wait_ge(neigh_copied, 1)
                for g in range(2):
                    with pe.Fori(0, BLOCKS) as b:
                        pe.wait_ge(heads_read, b + (g * BLOCKS + 1))
                        for h in range(4):
                            first = 4 * BLOCKS * g + h
                            pe.wait_ge(probs_ready, b * 4 + (first + 2))
                            for c in range(9):
                                if c < 8:
                                    if c >= 2:
                                        pe.wait_ge(probs_copied, b * 32 + (8 * first + c))
                                    else:
                                        pe.wait_ge(probs_copied, b * 32 + (8 * first + 1))
                                    for t in range(4):
                                        ins = pe.transpose(pe_turn[c % 2][:, 0, t * P:(t + 1) * P],
                                                           probs()[:, (4 * c + t) * P:(4 * c + t + 1) * P], ident[:, :])
                                    ins.then_inc(probs_turned, 1)
                                if c >= 1:
                                    pe.wait_ge(probs_copied, b * 32 + (8 * first + c + 1))
                                    for t in range(4):
                                        j = 4 * (c - 1) + t
                                        head = (4 * g + h) * D
                                        ins = pe.matmul(pe_sum[:, h * D:(h + 1) * D],
                                                        tiles[:, (c - 1) % TILE_BUFS, t * P:(t + 1) * P],
                                                        feats[:, j, head:head + D],
                                                        start=(j == 0), stop=(j == BLOCKS - 1))
                            ins.then_inc(heads_summed, 1)
            pe.wait_ge(verdict_ready, 1)

        @block.scalar
        def _(act):
            act.wait_ge(consts_zeroed, 2)
            for source, w, k in wb_loads:
                for half in range(2):
                    act.dma_start(wb[F * half:F * half + F, w:w + k, F * half:F * half + F], source)\
                        .then_inc(small_loaded, 16)
            for i, source in enumerate(rows_loads):
                act.dma_start(per_row[:, i, :], source.partition_broadcast(P)).then_inc(small_loaded, 16)

            def visit(stream, v, finish):
                for pos in range(STEPS):
                    tile = tiles[:, pos % TILE_BUFS, :]
                    if by_pe(stream, pos):
                        act.wait_ge(pe_turned, pe_no(stream, v, pos) + 1)
                        act.wait_ge(multiplied, step_no(stream, v, pos) + 1)
                        source = pe_turn[pos % TURN_BUFS][:, :, :].rearrange("p a n -> p (a n)")
                        if stream == HOP1:
                            act.activation(tile, source, ACT.Copy, accum_out=deg_part[:, pos:pos + 1])\
                                .then_inc(evacuated, 1)
                        else:
                            act.activation(tile, source, ACT.Copy).then_inc(evacuated, 1)
                    elif stream == HOP1:
                        act.wait_ge(dve_turned, dve_no(stream, v, pos) + 1)
                        if pos == 0:
                            act.wait_ge(deg_added, v)
                        if pos > 0 or not isinstance(v, int):
                            act.wait_ge(degrees_taken, dve_no(stream, v, pos))
                        act.activation(spare[:, :, :].rearrange("p b f -> p (b f)"), tile, ACT.Copy,
                                       accum_out=deg_part[:, pos:pos + 1]).then_inc(degrees_taken, 1)
                    if pos == 1 and not isinstance(v, int):
                        finish(v - 1)
                act.wait_ge(multiplied, step_no(stream, v, STEPS - 1) + 1 + TILE_BUFS)
                act.activation(sums[:, :], pe_sum[:, :], ACT.Copy).then_inc(sums_copied, 1)

            def product(stream, finish):
                visit(stream, 0, finish)
                with act.Fori(1, SB) as v:
                    visit(stream, v, finish)
                finish(SB - 1)

            def finish_hop1(v):
                act.wait_ge(rows_filled, rows_hop1(v) + 1)
                act.activation(rows_of(hop, superblock(HOP1, v)), pe_rows[:, :, :], ACT.Tanh).then_inc(rows_read, 1)

            def finish_hop2(v):
                act.wait_ge(rows_filled, rows_hop2(v) + 1)
                act.activation(second_hop[:, :, :], pe_rows[:, :, :], ACT.Tanh).then_inc(rows_read, 1)

            def finish_cheb1(v):
                act.wait_ge(rows_filled, rows_cheb1(v) + 1)
                act.activation(rows_of(t1, superblock(CHEB1, v)), pe_rows[:, :, :], ACT.Copy).then_inc(rows_read, 1)

            product(HOP1, finish_hop1)
            product(HOP2, finish_hop2)
            act.wait_ge(spread, SB * SB)
            for q in range(SB):
                act.activation(spread_sums[:, q, :], pe_turn[q // 2][:, q % 2, :], ACT.Copy).then_inc(spread_copied, 1)
            product(CHEB1, finish_cheb1)
            product(CHEB2, lambda v: None)
            product(CHEB3, lambda v: None)

            act.wait_ge(verdict_ready, 1)
            one = act.value_load(onehot[0:1, 0:1], min_val=0, max_val=1)
            with act.If(one == 0):
                for g in range(2):
                    with act.Fori(0, BLOCKS) as b:
                        for h in range(4):
                            first = 4 * BLOCKS * g + h
                            act.wait_ge(scores_ready, b * 4 + first + 1)
                            act.wait_ge(probs_turned, b * 32 + (8 * first + 1))
                            act.activation(probs(), scores(), ACT.Exp, bias=neg_max[:, h:h + 1],
                                           accum_out=weight_sum[:, h:h + 1]).then_inc(probs_ready, 1)
                            for c in range(8):
                                act.wait_ge(probs_turned, b * 32 + (8 * first + c + 2))
                                act.activation(tiles[:, c % TILE_BUFS, 0:HALF], pe_turn[c % 2][:, 0, :], ACT.Copy)\
                                    .then_inc(probs_copied, 1)
            act.wait_ge(verdict_ready, 1)

        @block.vector
        def _(dve):
            links = {"before": 0, "here": 0}
            loop = []

            def mark(ins):
                ins.then_inc(vec, 1)
                links["here"] += 1

            def join(apart=False):
                count = links["before"] + links["here"]
                if loop:
                    var, start, per = loop[0]
                    count = var * per + (count - start * per)
                if apart:
                    wait_apart(dve, vec, count, consts_zeroed)
                else:
                    dve.wait_ge(vec, count)

            def link(ins):
                mark(ins)
                join()

            def enter(var, start, per):
                links["before"] += links["here"]
                links["here"] = 0
                loop.append((var, start, per))

            def leave(turns):
                per = loop.pop()[2]
                assert links["here"] == per, f"a turn of the loop has {links['here']} links, not {per}"
                links["before"] += per * turns
                links["here"] = 0

            def inverse_root(y, v_in, t):
                link(dve.tensor_scalar(t.bitcast(U32), v_in.bitcast(U32), 1, None, ALU.logical_shift_right))
                link(dve.tensor_scalar(y.bitcast(I32), t.bitcast(I32), -1.0, float(0x5F3759DF), ALU.mult, ALU.add))
                for _ in range(3):
                    link(dve.tensor_tensor(t, y, y, ALU.mult))
                    link(dve.scalar_tensor_tensor(t, t, -0.5, v_in, ALU.mult, ALU.mult))
                    link(dve.scalar_tensor_tensor(y, t, 1.5, y, ALU.add, ALU.mult))

            def wide(a):
                return a.unsqueeze(2).to_broadcast([P, BPS, F])

            def for_all(i):
                return per_row[:, i, :].unsqueeze(1).to_broadcast([P, BPS, F])

            def norm(final):
                link(dve.tensor_reduce(rowsum[:, :], work[:, :, :], X, ALU.add))
                link(dve.tensor_scalar(rowsum[:, :], rowsum[:, :], -1.0 / F, None, ALU.mult))
                link(dve.tensor_tensor(work[:, :, :], work[:, :, :], wide(rowsum[:, :]), ALU.add))
                link(dve.tensor_tensor(square[:, :, :], work[:, :, :], work[:, :, :], ALU.mult))
                link(dve.tensor_reduce(rowsum[:, :], square[:, :, :], X, ALU.add))
                v = root_x[:, 0:BPS]
                link(dve.tensor_scalar(v, rowsum[:, :], 1.0 / F, EPS, ALU.mult, ALU.add))
                inverse_root(root_y[:, 0:BPS], v, root_t[:, 0:BPS])
                final(work[:, :, :], wide(root_y[:, 0:BPS]))

            def scan(stream, v, q, half):
                base = SCAN * half
                s = superblock(stream, v)
                wait_apart(dve, chunk_loaded[q], loaded(stream, v, q), consts_zeroed)
                for t in range(SCAN):
                    ins = dve.max(top8[:, t, :], ring[:, q, base + t, :])
                mark(ins)
                join(apart=True)
                for t in range(SCAN):
                    ins = dve.max_index(top8_at[:, t, :], top8[:, t, :], ring[:, q, base + t, :])
                ins.then_inc(scanned, 1)
                wait_apart(dve, scanned, scan_no(stream, v, q, half) + 1, consts_zeroed)
                mark(dve.tensor_copy(top2[:, bass.ds(s * BPS + base, SCAN), q, :], top8[:, :, 0:2]))
                mark(dve.tensor_copy(top_at[:, bass.ds(s * BPS + base, SCAN), q], top8_at[:, :, 0]))
                join(apart=True)

            def turn(stream, v):
                for pos in range(STEPS):
                    q, j = quarters(stream)[pos // BPS], pos % BPS
                    if by_pe(stream, pos):
                        continue
                    if j == 0:
                        dve.wait_ge(chunk_loaded[q], loaded(stream, v, q))
                    dve.wait_ge(multiplied, step_no(stream, v, pos) + 1)
                    if stream == HOP1 and pos >= TILE_BUFS:
                        dve.wait_ge(degrees_taken, dve_no(stream, v, pos) - TILE_BUFS + 1)
                    dve.transpose(tiles[:, pos % TILE_BUFS, :], ring_runs[:, q, :, j::BPS]).then_inc(dve_turned, 1)

            def stage(buf, s):
                dve.tensor_copy(staged_by_half(), split(rows_of(buf, s))).then_inc(staged, 1)

            def take_flip(count):
                dve.wait_ge(flip_filled, count + 1)
                source = pe_flip[:, :, :].rearrange("p b f -> p (b f)")
                dve.tensor_copy(paired[:, :], source).then_inc(flip_read, 1)

            def visits(body, per):
                body(0)
                with dve.Fori(1, SB) as v:
                    enter(v, 1, per)
                    body(v)
                    leave(SB - 1)

            dve.wait_ge(small_loaded, 16 * 12)
            dve.wait_ge(consts_zeroed, 3)
            dve.wait_ge(x_loaded, 16 * SB)
            mark(dve.tensor_tensor(wb[:, W_C0, :], wb[:, W_C0, :], wb[:, W_C2, :], ALU.subtract))
            link(dve.tensor_tensor(wb[:, W_C1, :], wb[:, W_C1, :], wb[:, W_C3, :], ALU.subtract))
            link(dve.tensor_scalar(wb[:, W_C2:W_C3 + 1, :], wb[:, W_C2:W_C3 + 1, :], 2.0, None, ALU.mult))

            def hop1(v):
                turn(HOP1, v)
                stage(x0, superblock(HOP1, v))
                scan(HOP1, v, NATURAL, 0)
                take_flip(flip_hop1(v))
                scan(HOP1, v, NATURAL, 1)
                dve.wait_ge(evacuated, pe_no(HOP1, v, BPS - 1) + 1 + TURN_BUFS)
                dve.tensor_tensor(deg[:, :], deg[:, :], deg_part[:, :], ALU.add).then_inc(deg_added, 1)
                dve.wait_ge(deg_added, v + 1)

            visits(hop1, 6)

            link(dve.tensor_scalar(root_x[:, :], deg[:, :], 1e-30, None, ALU.max))
            inverse_root(root_y[:, :], root_x[:, :], root_t[:, :])
            link(dve.tensor_scalar(root_t[:, :], deg[:, :], 0.0, None, ALU.is_gt))
            link(dve.tensor_tensor(dinv[:, :], root_y[:, :], root_t[:, :], ALU.mult))

            def norm_hop2(v):
                s = superblock(HOP2, v)
                wait_apart(dve, rows_read, rows_hop2(v) + 1, consts_zeroed)
                link(dve.tensor_tensor(work[:, :, :], second_hop[:, :, :], rows_of(x0, s), ALU.add))
                norm(lambda rows, factor: dve.tensor_tensor(staged_by_half(), split(rows), split(factor), ALU.mult)
                     .then_inc(staged, 1))
                dve.wait_ge(staged, 6 + 2 * v)
                link(dve.tensor_copy(split(rows_of(y1, s)), staged_by_half()))

            def scale_z(v):
                s = superblock(HOP2, v)
                wait_apart(dve, rows_filled, rows_gcn(v) + 1, consts_zeroed)
                factor = dinv[:, bass.ds(s * BPS, BPS)].unsqueeze(2).to_broadcast([P, BPS, F])
                dve.tensor_tensor(rows_of(z, s), pe_rows[:, :, :], factor, ALU.mult).then_inc(rows_read, 1)

            def hop2(v):
                first = isinstance(v, int)
                turn(HOP2, v)
                if first:
                    dve.wait_ge(rows_read, rows_hop1(SB - 1) + 1)
                else:
                    norm_hop2(v - 1)
                    take_flip(flip_gcn(v - 1))
                    scale_z(v - 1)
                stage(hop, superblock(HOP2, v))
                take_flip(flip_hop2(v))

            visits(hop2, 19)
            norm_hop2(SB - 1)
            take_flip(flip_gcn(SB - 1))
            scale_z(SB - 1)

            with dve.Fori(0, SB) as v:
                enter(v, 0, 18)
                for q in range(NATURAL):
                    for half in range(2):
                        scan(SPREAD, v, q, half)
                leave(SB)

            for q in range(SB):
                blocks = slice(q * BPS, (q + 1) * BPS)
                dve.wait_ge(rows_filled, rows_spread(q) + 1)
                dve.tensor_tensor(y2[:, blocks, :], pe_rows[:, :, :], z[:, blocks, :], ALU.add).then_inc(rows_read, 1)
            dve.wait_ge(rows_read, rows_spread(SB - 1) + 1)

            def wide_all(a):
                return a.unsqueeze(2).to_broadcast([P, BLOCKS, F])

            link(dve.tensor_tensor(y2[:, :, :], y2[:, :, :], wide_all(dinv[:, :]), ALU.mult))
            link(dve.tensor_tensor(y2[:, :, :], y2[:, :, :], per_row[:, 0, :].unsqueeze(1).to_broadcast([P, BLOCKS, F]), ALU.add))
            link(dve.scalar_tensor_tensor(y2[:, :, :], y2[:, :, :], 0.0, y1[:, :, :], ALU.max, ALU.add))
            squares = buf_b
            link(dve.tensor_reduce(root_t[:, :], y2[:, :, :], X, ALU.add))
            link(dve.tensor_scalar(root_t[:, :], root_t[:, :], -1.0 / F, None, ALU.mult))
            link(dve.tensor_tensor(y2[:, :, :], y2[:, :, :], wide_all(root_t[:, :]), ALU.add))
            link(dve.tensor_tensor(squares[:, :, :], y2[:, :, :], y2[:, :, :], ALU.mult))
            link(dve.tensor_reduce(root_x[:, :], squares[:, :, :], X, ALU.add))
            link(dve.tensor_scalar(root_x[:, :], root_x[:, :], 1.0 / F, EPS, ALU.mult, ALU.add))
            inverse_root(root_y[:, :], root_x[:, :], root_t[:, :])
            dve.tensor_tensor(y2[:, :, :], y2[:, :, :], wide_all(root_y[:, :]), ALU.mult).then_inc(y2_ready, 1)
            dve.wait_ge(y2_ready, 1)

            def find_leads():
                for b in range(BLOCKS):
                    ins = dve.max(best[:, b, :], top2[:, b, :, :].rearrange("p q k -> p (q k)"))
                link(ins)
                largest = best[:, :, 0:1].to_broadcast([P, BLOCKS, SB])
                for q in range(SB):
                    mark(dve.tensor_scalar(top_at[:, :, q], top_at[:, :, q], float(q * QUARTER), None, ALU.add))
                link(dve.tensor_tensor(hit[:, :, :], top2[:, :, :, 0], largest, ALU.is_equal))
                link(dve.tensor_tensor(hit[:, :, :], hit[:, :, :], top_at[:, :, :], ALU.mult))
                link(dve.tensor_reduce(neighbour[:, :], hit[:, :, :], X, ALU.add))
                link(dve.tensor_copy(neighbour_u[:, :], neighbour[:, :]))
                for k in range(2):
                    link(dve.tensor_scalar(lead[:, k, :], best[:, :, k], -1.0, 1.0, ALU.mult, ALU.add))
                    link(dve.tensor_scalar(lead[:, k, :], lead[:, k, :], NEG, None, ALU.mult))
                link(dve.tensor_tensor(lead[:, 1, :], lead[:, 1, :], lead[:, 0, :], ALU.subtract))
                link(dve.tensor_scalar(lead[:, 2, :], lead[:, 0, :], 2.0 ** -20, None, ALU.mult))
                link(dve.scalar_tensor_tensor(lead[:, 2, :], lead[:, 2, :], -1.0, lead[:, 2, :], ALU.mult, ALU.max))
                link(dve.scalar_tensor_tensor(lead[:, 2, :], lead[:, 1, :], 0.99, lead[:, 2, :], ALU.mult, ALU.add))
                link(dve.tensor_reduce(worst[:, 0:1], lead[:, 2, :], X, ALU.max))

            def keep_cheb1(v):
                wait_apart(dve, flip_filled, filt_cheb1(v) + 1, consts_zeroed)
                dve.tensor_copy(rows_of(filtered, superblock(CHEB1, v)), pe_flip[:, :, :]).then_inc(flip_read, 1)

            def cheb1(v):
                turn(CHEB1, v)
                if not isinstance(v, int):
                    keep_cheb1(v - 1)
                stage(y2, superblock(CHEB1, v))
                take_flip(flip_cheb1(v))
                if isinstance(v, int):
                    find_leads()

            visits(cheb1, 0)
            keep_cheb1(SB - 1)
            dve.wait_ge(flip_read, filt_cheb1(SB - 1) + 1)

            def keep_cheb2(v):
                s = superblock(CHEB2, v)
                wait_apart(dve, rows_filled, rows_cheb2(v) + 1, consts_zeroed)
                dve.scalar_tensor_tensor(rows_of(t2, s), pe_rows[:, :, :], 2.0, rows_of(y2, s),
                                         ALU.mult, ALU.subtract).then_inc(rows_read, 1)
                wait_apart(dve, flip_filled, filt_cheb2(v) + 1, consts_zeroed)
                dve.tensor_tensor(rows_of(filtered, s), rows_of(filtered, s), pe_flip[:, :, :], ALU.add)\
                    .then_inc(flip_read, 1)

            def cheb2(v):
                if not isinstance(v, int):
                    keep_cheb2(v - 1)
                turn(CHEB2, v)

            visits(cheb2, 0)
            keep_cheb2(SB - 1)
            dve.wait_ge(flip_read, filt_cheb2(SB - 1) + 1)

            def norm_cheb3(v):
                s = superblock(CHEB3, v)
                wait_apart(dve, flip_filled, filt_cheb3(v) + 1, consts_zeroed)
                dve.tensor_tensor(work[:, :, :], rows_of(filtered, s), pe_flip[:, :, :], ALU.add).then_inc(flip_read, 1)
                dve.wait_ge(flip_read, filt_cheb3(v) + 1)
                link(dve.tensor_tensor(work[:, :, :], work[:, :, :], rows_of(y2, s), ALU.add))
                norm(lambda rows, factor: dve.tensor_tensor(staged_by_half(), split(rows), split(factor), ALU.mult)
                     .then_inc(staged, 1))
                dve.wait_ge(staged, 17 + v)
                link(dve.tensor_copy(split(rows_of(y3, s)), staged_by_half()))
                take_flip(flip_gat(v))
                wait_apart(dve, rows_filled, rows_gat(v) + 1, consts_zeroed)
                dve.tensor_copy(rows_of(feats, s), pe_rows[:, :, :]).then_inc(rows_read, 1)
                dve.wait_ge(rows_read, rows_gat(v) + 1)
                for i in range(2):
                    link(dve.tensor_tensor(square[:, :, :], rows_of(feats, s), for_all(1 + i), ALU.mult))
                    link(dve.tensor_reduce(att[:, i, bass.ds(s * BPS, BPS), :],
                                           square[:, :, :].rearrange("p b (h d) -> p b h d", h=H), X, ALU.add))

            def cheb3(v):
                turn(CHEB3, v)
                if not isinstance(v, int):
                    norm_cheb3(v - 1)

            visits(cheb3, 23)
            norm_cheb3(SB - 1)

            for i in range(2):
                att_i = att[:, i, :, :].rearrange("p b h -> p (b h)")
                ins = dve.tensor_reduce(worst[:, 1 + i:2 + i], att_i, X, ALU.max, apply_absolute_value=True)
            ins.then_inc(worst_found, 1)
            dve.wait_ge(worst_reduced, 1)
            link(dve.tensor_tensor(verdict[:, 0:1], worst_all[:, 1:2], worst_all[:, 2:3], ALU.add))
            link(dve.tensor_scalar(verdict[:, 0:1], verdict[:, 0:1], 2.0, 128.0, ALU.mult, ALU.add))
            link(dve.tensor_tensor(verdict[:, 1:2], verdict[:, 0:1], worst_all[:, 0:1], ALU.add))
            dve.tensor_scalar(onehot[:, :], verdict[:, 1:2], 0.0, None, ALU.is_lt).then_inc(verdict_ready, 1)
            dve.wait_ge(verdict_ready, 1)
            one = dve.value_load(onehot[0:1, 0:1], min_val=0, max_val=1)

            def last_norm(s):
                blocks = slice(s * BPS, (s + 1) * BPS)
                dve.wait_ge(out_ready, s)
                link(dve.tensor_tensor(work[:, :, :], attended[:, blocks, :], for_all(3), ALU.add))
                link(dve.scalar_tensor_tensor(work[:, :, :], work[:, :, :], 0.0, y3[:, blocks, :], ALU.max, ALU.add))
                norm(lambda rows, factor: dve.tensor_tensor(attended[:, blocks, :], rows, factor, ALU.mult)
                     .then_inc(out_ready, 1))

            taken = links["before"] + links["here"]
            with dve.If(one == 1):
                for s in range(SB):
                    dve.wait_ge(gathered[s], 16 * BPS)
                    last_norm(s)
            links.update(before=taken, here=0)
            with dve.Else():
                dve.wait_ge(neigh_turned, 1)
                dve.tensor_copy(staged_rows[:, :, :].rearrange("p b f -> p (b f)")[:, 0:2 * P],
                                pe_turn[0][:, 0, 0:2 * P]).then_inc(neigh_copied, 1)
                for g in range(2):
                    dve.wait_ge(neigh_loaded, 64 * (g + 1))
                    with dve.Fori(0, BLOCKS) as b:
                        enter(b, 0, 19)
                        dve.wait_ge(mask_loaded, b * 16 + (g * BLOCKS + 1) * 16)
                        link(dve.tensor_scalar(mask(), mask(), -1.0, 1.0, ALU.mult, ALU.add))
                        link(dve.tensor_scalar(mask(), mask(), NEG, None, ALU.mult))
                        for h in range(4):
                            head = 4 * g + h
                            first = 4 * BLOCKS * g + h
                            dve.wait_ge(probs_ready, b * 4 + (first + 1))
                            link(dve.tensor_scalar(scores(), neigh_terms(h), att[:, 0, bass.ds(b, 1), head],
                                                   None, ALU.add))
                            link(dve.scalar_tensor_tensor(scores(), scores(), 0.2, scores(), ALU.mult, ALU.max))
                            link(dve.tensor_tensor(scores(), scores(), mask(), ALU.add))
                            link(dve.tensor_reduce(neg_max[:, h:h + 1], scores(), X, ALU.max))
                            dve.tensor_scalar(neg_max[:, h:h + 1], neg_max[:, h:h + 1], -1.0, None, ALU.mult)\
                                .then_inc(scores_ready, 1)
                        dve.wait_ge(heads_summed, b * 4 + (4 * BLOCKS * g + 4))
                        link(dve.reciprocal(weight_sum[:, :], weight_sum[:, :]))
                        dst = attended[:, bass.ds(b, 1), 4 * g * D:4 * (g + 1) * D].rearrange("p b (h d) -> p (b h) d", h=4)
                        dve.tensor_tensor(dst, pe_sum[:, 0:4 * D].rearrange("p (h d) -> p h d", h=4),
                                                 weight_sum[:, :].unsqueeze(2).to_broadcast([P, 4, D]), ALU.mult)\
                            .then_inc(heads_read, 1)
                        leave(BLOCKS)
                dve.wait_ge(attended_back, 16 * SB)
                for s in range(SB):
                    last_norm(s)
            dve.wait_ge(verdict_ready, 1)


_INS = ['x', 'adj', 'L0_gnn_W', 'L1_gnn_W', 'L1_gnn_b', 'L2_gnn_weight', 'L3_gnn_W',
        'L3_gnn_att_self', 'L3_gnn_att_neigh', 'L3_gnn_bias']
_OUTS = [((4096, 64), 'float32')]


def kernel(**inputs):
    import numpy as _np
    import concourse.bacc as _bacc
    from concourse import mybir as _mybir
    from concourse.bass_utils import run_bass_kernel_spmd as _run

    nc = _bacc.Bacc("TRN2", target_bir_lowering=False, num_devices=1)
    arrays, args = {}, []
    for name in _INS:
        a = _np.ascontiguousarray(inputs[name])
        arrays[f"in_{name}_dram"] = a
        args.append(nc.dram_tensor(f"in_{name}_dram", a.shape, _mybir.dt.from_np(a.dtype), kind="ExternalInput").ap())
    for i, (shape, dtype) in enumerate(_OUTS):
        dt = _mybir.dt.from_np(_np.dtype(dtype))
        args.append(nc.dram_tensor(f"out_{i}_dram", shape, dt, kind="ExternalOutput").ap())
    build(nc, *args)
    r = _run(nc, [arrays], core_ids=[0])
    return r.results[0]["out_0_dram"]
```

```python
from contextlib import ExitStack

import concourse.bass as bass
from concourse import mybir

F32 = mybir.dt.float32
U32 = mybir.dt.uint32
I32 = mybir.dt.int32
ALU = mybir.AluOpType
ACT = mybir.ActivationFunctionType
X = mybir.AxisListType.X

P = 128
N, F = 4096, 64
H, D = 8, 8
BLOCKS = N // P
SB = 4
BPS = BLOCKS // SB
QUARTER = N // SB
HALF = QUARTER // 2
STEPS = BLOCKS
TURN_BUFS = 2
TILE_BUFS = 4
SCAN = 4
FAR = 5
NEAR = BPS - FAR
RUN = QUARTER // 4
NATURAL = SB - 1
OTHERS = (SB - 1) * BPS
PIECES = 4
REAR = STEPS - BPS + TILE_BUFS
BY_PE = range(STEPS - 2 * BPS, STEPS - BPS)
EPS = 1e-5
NEG = -1e10

HOP1, HOP2, SPREAD, CHEB1, CHEB2, CHEB3 = range(6)
TURNED = {HOP1: 0, HOP2: 1, CHEB1: 2, CHEB2: 3, CHEB3: 4}

W_H1A, W_H1X, W_H2A, W_H2X, W_GCN, W_C0, W_C1, W_C2, W_C3, W_GAT, W_ONE = range(11)


def superblock(stream, v):
    return v if stream % 2 == 0 else SB - 1 - v


def quarters(stream):
    if stream == SPREAD:
        return [0, 1, 2, 3]
    return [2, 1, 3, 0] if stream == CHEB2 else [0, 1, 3, 2]


def loaded(stream, v, q):
    if q == NATURAL:
        first = 1 + (SB - 1) * stream
    else:
        first = (1, 4, 8, 12, 15, 18)[stream]
    return 16 * PIECES * (first + v)


def step_no(stream, v, pos):
    return STEPS * SB * TURNED[stream] + STEPS * v + pos


def pe_no(stream, v, pos):
    return BPS * SB * TURNED[stream] + BPS * v + pos % BPS


def dve_no(stream, v, pos):
    return OTHERS * SB * TURNED[stream] + OTHERS * v + (pos if pos < BY_PE[0] else pos - BPS)


def user_before(stream, v, pos):
    return step_no(stream, v, pos) - TILE_BUFS - (BPS if 0 <= pos - BY_PE[-1] - 1 < TILE_BUFS else 0)


def scan_no(stream, v, q, half):
    if stream == SPREAD:
        return SB + far_no(v, q)
    return v if stream == HOP1 else SB + (SB - 1) * SB + v


def far_no(v, q):
    return (SB - 1) * v + q


def rows_hop1(v):
    return 1 + v


def rows_hop2(v):
    return 5 + 2 * v


def rows_gcn(v):
    return 6 + 2 * v


def rows_spread(q):
    return 13 + q


def rows_cheb1(v):
    return 17 + v


def rows_cheb2(v):
    return 21 + v


def rows_gat(v):
    return 25 + v


def flip_hop1(v):
    return 1 + v


def flip_hop2(v):
    return 5 + 2 * v


def flip_gcn(v):
    return 6 + 2 * v


def flip_cheb1(v):
    return 13 + 2 * v


def filt_cheb1(v):
    return 14 + 2 * v


def filt_cheb2(v):
    return 21 + v


def filt_cheb3(v):
    return 25 + 2 * v


def flip_gat(v):
    return 26 + 2 * v


def wait_apart(eng, semaphore, value, holds):
    if isinstance(value, int):
        eng.wait_ge(semaphore, value)
        return
    value = eng.to_reg(value)
    eng.wait_ge(holds, 1)
    eng.wait_ge(semaphore, value)


def build(nc, x, adj, w_hop, w_gcn, b_gcn, w_cheb, w_gat, att_self, att_neigh, b_gat, out):
    ctx = ExitStack()
    with ctx:
        def sb(name, shape, dt=F32):
            return ctx.enter_context(nc.sbuf_tensor(name, shape, dt))

        def ps(name, shape):
            return ctx.enter_context(nc.psum_tensor(name, shape, F32))

        def sem(name):
            return ctx.enter_context(nc.semaphore(name))

        feats_dram = nc.dram_tensor("feats_scratch", [N, F], F32, kind="Internal")
        att_dram = nc.dram_tensor("att_scratch", [2, N, H], F32, kind="Internal")
        neigh_dram = nc.dram_tensor("neigh_scratch", [BLOCKS * H, P], F32, kind="Internal")

        ring = sb("ring", [P, SB, BPS, QUARTER])
        tiles = sb("tiles", [P, TILE_BUFS, QUARTER])
        pe_tiles = sb("pe_tiles", [P, TURN_BUFS, QUARTER])
        buf_a = sb("buf_a", [P, BLOCKS, F])
        buf_b = sb("buf_b", [P, BLOCKS, F])
        buf_c = sb("buf_c", [P, BLOCKS, F])
        buf_d = sb("buf_d", [P, BLOCKS, F])
        x0 = y2 = buf_a
        hop = buf_b
        t2 = attended = buf_b
        y1 = t1 = y3 = buf_c
        z = filtered = feats = buf_d
        spread_sums = buf_b[:, :, :].rearrange("p b f -> p (b f)").rearrange("p (q n) -> p q n", q=SB)

        ident = sb("ident", [P, P])
        wb = sb("wb", [P, 11, P])
        per_row = sb("per_row", [P, 4, F])
        sums = sb("sums", [P, HALF])
        staged_rows = sb("staged_rows", [P, BPS, F])
        paired = sb("paired", [P, HALF])
        second_hop = sb("second_hop", [P, BPS, F])
        spare = sb("spare", [P, 2 * BPS, F])
        work, square = spare[:, 0:BPS, :], spare[:, BPS:2 * BPS, :]
        rowsum = sb("rowsum", [P, BPS])
        root_t = sb("root_t", [P, BLOCKS])
        root_y = sb("root_y", [P, BLOCKS])
        root_x = sb("root_x", [P, BLOCKS])
        deg_part = sb("deg_part", [P, BLOCKS])
        deg = sb("deg", [P, BLOCKS])
        dinv = sb("dinv", [P, BLOCKS])
        top8 = sb("top8", [P, SCAN, 8])
        top8_at = sb("top8_at", [P, SCAN, 8], U32)
        top2 = sb("top2", [P, BLOCKS, SB, 2])
        top_at = sb("top_at", [P, BLOCKS, SB])
        best = sb("best", [P, BLOCKS, 8])
        far8, far_sum = best[:, 0:FAR, :], best[:, FAR, 0:FAR]
        column_no = pe_tiles[:, 0, :]
        far_tiles = [tiles[:, t, :] for t in range(TILE_BUFS)] + [pe_tiles[:, 1, :]]
        hit = sb("hit", [P, BLOCKS, SB])
        neighbour = sb("neighbour", [P, BLOCKS])
        neighbour_u = sb("neighbour_u", [P, BLOCKS], U32)
        lead = sb("lead", [P, 3, BLOCKS])
        att = second_hop[:, :, :].rearrange("p b f -> p (b f)")\
            .rearrange("p (i b h) -> p i b h", i=2, b=BLOCKS)
        worst = sb("worst", [P, 3])
        worst_all = sb("worst_all", [P, 3])
        verdict = sb("verdict", [P, 2])
        onehot = sb("onehot", [P, 1], I32)
        neg_max = sb("neg_max", [P, 4])
        weight_sum = sb("weight_sum", [P, 4])

        pe_turn = [ps(f"pe_turn{i}", [P, 2, HALF]) for i in range(TURN_BUFS)]
        pe_sum = ps("pe_sum", [P, HALF])
        pe_rows = ps("pe_rows", [P, BPS, F])
        pe_flip = ps("pe_flip", [P, BPS, F])

        chunk_loaded = [sem(f"chunk_loaded{q}") for q in range(SB)]
        x_loaded = sem("x_loaded")
        small_loaded = sem("small_loaded")
        consts_zeroed = sem("consts_zeroed")
        weights_zeroed = sem("weights_zeroed")
        consts_ready = sem("consts_ready")
        pe_turned = sem("pe_turned")
        evacuated = sem("evacuated")
        dve_turned = sem("dve_turned")
        degrees_taken = sem("degrees_taken")
        multiplied = sem("multiplied")
        sums_copied = sem("sums_copied")
        rows_filled = sem("rows_filled")
        rows_read = sem("rows_read")
        flip_filled = sem("flip_filled")
        flip_read = sem("flip_read")
        staged = sem("staged")
        scanned = sem("scanned")
        numbers_ready = sem("numbers_ready")
        far_found = sem("far_found")
        compared = sem("compared")
        numbered = sem("numbered")
        far_summed = sem("far_summed")
        far_taken = sem("far_taken")
        deg_added = sem("deg_added")
        spread = sem("spread")
        spread_copied = sem("spread_copied")
        y2_ready = sem("y2_ready")
        vec = sem("vec")
        feats_stored = sem("feats_stored")
        worst_found = sem("worst_found")
        worst_reduced = sem("worst_reduced")
        verdict_ready = sem("verdict_ready")
        gathered = [sem(f"gathered{s}") for s in range(SB)]
        out_ready = sem("out_ready")
        out_stored = sem("out_stored")
        att_stored = sem("att_stored")
        in_order = sem("in_order")
        neigh_turned = sem("neigh_turned")
        neigh_copied = sem("neigh_copied")
        neigh_stored = sem("neigh_stored")
        neigh_loaded = sem("neigh_loaded")
        mask_loaded = sem("mask_loaded")
        scores_ready = sem("scores_ready")
        probs_ready = sem("probs_ready")
        probs_turned = sem("probs_turned")
        probs_copied = sem("probs_copied")
        heads_summed = sem("heads_summed")
        heads_read = sem("heads_read")
        attended_stored = sem("attended_stored")
        attended_back = sem("attended_back")

        x_rows = x.rearrange("(s p m) f -> s p m f", p=P, m=BPS)
        out_rows = out.rearrange("(s p m) f -> s p m f", p=P, m=BPS)
        feats_rows = feats_dram[:, :].rearrange("(s p m) f -> s p m f", p=P, m=BPS)
        ring_flat = ring[:, :, :, :].rearrange("p q t n -> p q (t n)")
        ring_runs = ring_flat.rearrange("p q (k e) -> p q k e", e=RUN)

        def rows_of(buf, s):
            return buf[:, bass.ds(s * BPS, BPS), :]

        def split(a):
            return a.rearrange("p (h t) f -> p h t f", h=2)

        def staged_by_half():
            return staged_rows[:, :, :].rearrange("p (t h) f -> p h t f", h=2)

        def pairs(t):
            return lambda a: a[:, t::BPS // 2, :]

        def spread_bank(q):
            return pe_turn[q // 2][:, q % 2, :].rearrange("p (b f) -> p b f", f=F)

        wb_loads = [(w_hop.rearrange("k (a f) g -> f (k a) g", a=2), W_H1A, 4),
                    (w_gcn.rearrange("f (k g) -> f k g", k=1), W_GCN, 1),
                    (w_cheb.rearrange("k f g -> f k g"), W_C0, 4),
                    (w_gat.rearrange("f (k g) -> f k g", k=1), W_GAT, 1)]
        rows_loads = [b_gcn, att_self.rearrange("h d -> (h d)"), att_neigh.rearrange("h d -> (h d)"),
                      b_gat.rearrange("h d -> (h d)")]

        flat_ring = ring[:, :, :, :].rearrange("p q t n -> p (q t n)")

        def neigh_terms(h):
            return flat_ring[:, h * N:(h + 1) * N]

        def mask():
            return flat_ring[:, 4 * N:5 * N]

        def scores():
            return flat_ring[:, 5 * N:6 * N]

        def probs():
            return flat_ring[:, 6 * N:7 * N]

        block = ctx.enter_context(nc.Block())

        @block.sync
        def _(sp):
            def load(stream, s, q):
                cols = slice(q * QUARTER, (q + 1) * QUARTER)
                for i in range(PIECES):
                    if q == NATURAL or stream == SPREAD:
                        rows = adj[bass.ds(s * QUARTER, QUARTER), cols].rearrange("(p m) j -> p m j", m=BPS)
                        two = slice(i * BPS // PIECES, (i + 1) * BPS // PIECES)
                        ins = sp.dma_start(ring[:, q, two, :], rows[:, two, :])
                    else:
                        rows = adj[bass.ds(s * QUARTER + i * RUN, RUN), cols]
                        ins = sp.dma_start(ring_runs[:, q, i::PIECES, :],
                                           rows.rearrange("(c m) (a e) -> a c m e", m=BPS, e=RUN))
                    ins.then_inc(chunk_loaded[q], 16)

            for q in quarters(HOP1):
                load(HOP1, 0, q)
                if q == 0:
                    for s in range(SB):
                        sp.dma_start(rows_of(x0, s), x_rows[s]).then_inc(x_loaded, 16)

            def reload(stream, v):
                for r, q in enumerate(quarters(stream)):
                    if stream != SPREAD and q == NATURAL:
                        wait_apart(sp, pe_turned, pe_no(stream, v - 1, 0) + BPS, consts_zeroed)
                    elif stream != SPREAD:
                        wait_apart(sp, dve_turned, dve_no(stream, v - 1, BPS * r) + BPS, consts_zeroed)
                    else:
                        wait_apart(sp, spread, SB * (v - 1) + r + 1, consts_zeroed)
                    if stream in ((HOP1, CHEB1) if q == NATURAL else (SPREAD,)):
                        wait_apart(sp, scanned, scan_no(stream, v - 1, q, 1) + 1, consts_zeroed)
                    if stream == SPREAD and q != NATURAL:
                        wait_apart(sp, compared, FAR * (far_no(v - 1, q) + 1), consts_zeroed)
                    load(stream, superblock(stream, v), q)

            for stream in range(6):
                if stream == HOP2:
                    sp.wait_ge(scanned, scan_no(HOP1, SB, NATURAL, 0))
                if stream == CHEB2:
                    sp.wait_ge(scanned, scan_no(CHEB1, SB, NATURAL, 1))
                if stream == SPREAD:
                    for q in range(NATURAL):
                        sp.wait_ge(dve_turned, BPS * q + dve_no(HOP2, SB - 1, 0) + BPS)
                        load(SPREAD, superblock(SPREAD, 0), q)
                if stream == CHEB1:
                    for q in range(NATURAL):
                        sp.wait_ge(spread, SB * (SB - 1) + q + 1)
                        sp.wait_ge(scanned, scan_no(SPREAD, SB - 1, q, 1) + 1)
                        sp.wait_ge(compared, FAR * (far_no(SB - 1, q) + 1))
                        load(CHEB1, superblock(CHEB1, 0), q)
                with sp.Fori(1, SB) as v:
                    reload(stream, v)
            for v in range(SB):
                s = superblock(CHEB3, v)
                sp.wait_ge(rows_read, rows_gat(v) + 1)
                sp.dma_start(feats_rows[s], rows_of(feats, s)).then_inc(feats_stored, 16)
            sp.wait_ge(feats_stored, 16 * SB)

            sp.wait_ge(verdict_ready, 1)
            one = sp.value_load(onehot[0:1, 0:1], min_val=0, max_val=1)
            with sp.If(one == 0):
                for i in range(2):
                    for s in range(SB):
                        sp.dma_start(att_dram[i].rearrange("(s p m) h -> s p m h", p=P, m=BPS)[s],
                                     att[:, i, s * BPS:(s + 1) * BPS, :]).then_inc(att_stored, 16)
                sp.wait_ge(att_stored, 16 * 2 * SB)
                sp.dma_start(feats[:, :, :], feats_dram[:, :].rearrange("(b p) f -> p b f", p=P)).then_inc(in_order, 16)
                for i in range(2):
                    sp.dma_start(att[:, i, :, :], att_dram[i].rearrange("(b p) h -> p b h", p=P)).then_inc(in_order, 16)
                sp.wait_ge(neigh_copied, 1)
                sp.dma_start(neigh_dram[:, :].rearrange("(c b) p -> b c p", c=2),
                             staged_rows[:, :, :].rearrange("p b f -> p (b f)")[:, 0:2 * P]
                             .rearrange("p (c n) -> p c n", c=2)).then_inc(neigh_stored, 16)
                sp.wait_ge(neigh_stored, 16)
                neigh_all = neigh_dram[:, :].rearrange("(b h) p -> h b p", h=H)
                for g in range(2):
                    sp.wait_ge(heads_read, g * BLOCKS + 1)
                    for h in range(4):
                        sp.dma_start(neigh_terms(h).rearrange("p (b n) -> p b n", b=BLOCKS),
                                     neigh_all[4 * g + h].partition_broadcast(P)).then_inc(neigh_loaded, 16)
                    with sp.Fori(0, BLOCKS) as b:
                        wait_apart(sp, heads_read, b + (g * BLOCKS + 1), consts_zeroed)
                        sp.dma_start(mask(), adj[bass.ds(b * P, P), :]).then_inc(mask_loaded, 16)
                        wait_apart(sp, mask_loaded, b * 16 + (g * BLOCKS + 1) * 16, consts_zeroed)
                sp.wait_ge(heads_read, 2 * BLOCKS + 1)
                sp.dma_start(feats_dram[:, :].rearrange("(b p) f -> p b f", p=P), attended[:, :, :])\
                    .then_inc(attended_stored, 16)
                sp.wait_ge(attended_stored, 16)
                for s in range(SB):
                    sp.dma_start(rows_of(attended, s), feats_rows[s]).then_inc(attended_back, 16)
            for s in range(SB):
                sp.wait_ge(out_ready, s + 1)
                sp.dma_start(out_rows[s], rows_of(attended, s)).then_inc(out_stored, 16)
            sp.wait_ge(out_stored, 16 * SB)

        @block.gpsimd
        def _(pool):
            pool.memset(ident[:, :], 0.0).then_inc(consts_zeroed, 1)
            pool.memset(wb[:, W_ONE, :], 0.0).then_inc(consts_zeroed, 1)
            pool.memset(lead[:, 0, :], 0.0).then_inc(evacuated, TURN_BUFS)
            pool.memset(lead[:, 1, :], 0.0).then_inc(multiplied, TILE_BUFS)
            for i, count in enumerate((rows_filled, rows_read, flip_filled, flip_read, heads_read,
                                       probs_ready, probs_turned, probs_copied)):
                pool.memset(lead[:, 2, i:i + 1], 0.0).then_inc(count, 1)
            pool.memset(deg[:, :], 1.0).then_inc(consts_zeroed, 1)
            pool.wait_ge(consts_zeroed, 2)
            pool.affine_select(out=ident[:, :], in_=ident[:, :], compare_op=ALU.not_equal, fill=1.0,
                               base=0, pattern=[[-1, P]], channel_multiplier=1).then_inc(consts_ready, 1)
            pool.affine_select(out=wb[:, W_ONE, :], in_=wb[:, W_ONE, :], compare_op=ALU.not_equal, fill=1.0,
                               base=0, pattern=[[-1, P]], channel_multiplier=1).then_inc(consts_ready, 1)

            pool.wait_ge(multiplied, step_no(CHEB1, 0, 0) + TILE_BUFS)
            pool.iota(column_no, [[1, QUARTER]], base=0, channel_multiplier=0, allow_small_or_imprecise_dtypes=True)\
                .then_inc(numbers_ready, 1)
            pool.wait_ge(numbers_ready, 1)

            def far_numbers(v):
                for q in range(NATURAL):
                    for t in range(FAR):
                        pool.wait_ge(compared, FAR * far_no(v, q) + t + 1)
                        pool.tensor_tensor(far_tiles[t], far_tiles[t], column_no, ALU.mult).then_inc(numbered, 1)

            with pool.Fori(0, SB) as v:
                far_numbers(v)

            pool.wait_ge(worst_found, 1)
            pool.partition_all_reduce(worst_all[:, :], worst[:, :], P, bass.bass_isa.ReduceOp.max)\
                .then_inc(worst_reduced, 1)
            pool.wait_ge(verdict_ready, 1)
            one = pool.value_load(onehot[0:1, 0:1], min_val=0, max_val=1)
            with pool.If(one == 1):
                pool.wait_ge(feats_stored, 16 * SB)
                for b in range(BLOCKS):
                    pool.indirect_dma_start(attended[:, b, :], None, feats_dram[:, :],
                                            bass.IndirectOffsetOnAxis(neighbour_u[:, b:b + 1], 0))\
                        .then_inc(gathered[b // BPS], 16)
            pool.wait_ge(verdict_ready, 1)

        @block.tensor
        def _(pe):
            def turn(stream, v, pos):
                q, j = quarters(stream)[pos // BPS], pos % BPS
                n = pe_no(stream, v, pos)
                if j == 0:
                    pe.wait_ge(chunk_loaded[q], loaded(stream, v, q))
                pe.wait_ge(evacuated, n + 1)
                buf = pe_turn[pos % TURN_BUFS]
                for t in range(BPS):
                    ins = pe.transpose(buf[:, t // 4, t % 4 * P:(t % 4 + 1) * P],
                                       ring[:, q, t, j::BPS], ident[:, :])
                ins.then_inc(pe_turned, 1)

            def multiply(stream, v, pos, rows, ready):
                q = quarters(stream)[pos // BPS]
                if pos in BY_PE:
                    pe.wait_ge(evacuated, pe_no(stream, v, pos) + 1 + TURN_BUFS)
                else:
                    pe.wait_ge(dve_turned, dve_no(stream, v, pos) + 1)
                if pos == 0:
                    pe.wait_ge(sums_copied, SB * TURNED[stream] + v)
                if pos % BPS == 0 and isinstance(v, int) and ready is not None:
                    sem_, first = ready
                    finished = SB - 1 - q if stream == CHEB2 else q
                    pe.wait_ge(sem_, first + finished + 1)
                tile = pe_tiles[:, pos % TURN_BUFS] if pos in BY_PE else tiles[:, pos % TILE_BUFS]
                for half in range(2):
                    ins = pe.matmul(pe_sum[F * half:F * half + F, :], rows[:, BPS * q + pos % BPS, :],
                                    tile[:, half * HALF:(half + 1) * HALF],
                                    start=(pos == 0), stop=(pos == STEPS - 1))
                ins.then_inc(multiplied, 1)

            def project(bank, paired_terms, count):
                filled, read = (rows_filled, rows_read) if bank is pe_rows else (flip_filled, flip_read)
                pe.wait_ge(read, count)
                for t in range(BPS // 2):
                    for i, (source, w) in enumerate(paired_terms):
                        ins = pe.matmul(pairs(t)(bank), source[:, t * P:(t + 1) * P],
                                        wb[:, w, :].rearrange("p (h f) -> p h f", h=2),
                                        start=(i == 0), stop=(i == len(paired_terms) - 1))
                ins.then_inc(filled, 1)

            def flip(turn_no, count):
                pe.wait_ge(staged, turn_no + 1)
                pe.wait_ge(flip_read, count)
                for t in range(BPS // 2):
                    pair = [a[:, 2 * t:2 * t + 2, :].rearrange("p b f -> p (b f)") for a in (pe_flip, staged_rows)]
                    ins = pe.transpose(pair[0], pair[1], ident[:, :])
                ins.then_inc(flip_filled, 1)

            def visit(stream, v, rows, ready, finish, extra, pending=None):
                first = isinstance(v, int)
                for pos in range(STEPS):
                    if pos in BY_PE:
                        turn(stream, v, pos)
                    if pos >= 1:
                        multiply(stream, v, pos - 1, rows, ready)
                    if pos == 2 and not first:
                        finish(v - 1)
                    elif pos == 2 and pending is not None:
                        pending()
                    for at, needs_before, act in extra:
                        if at == pos and not (first and needs_before):
                            act(v)
                multiply(stream, v, STEPS - 1, rows, ready)

            def product(stream, rows, ready, finish, extra=(), pending=None):
                visit(stream, 0, rows, ready, finish, extra, pending)
                with pe.Fori(1, SB) as v:
                    visit(stream, v, rows, ready, finish, extra)
                return lambda: finish(SB - 1)

            def sums_ready(stream, v):
                pe.wait_ge(sums_copied, SB * TURNED[stream] + v + 1)

            pe.wait_ge(consts_ready, 2)

            def finish_hop1(v):
                sums_ready(HOP1, v)
                pe.wait_ge(flip_read, flip_hop1(v) + 1)
                project(pe_rows, [(sums, W_H1A), (paired, W_H1X)], rows_hop1(v))

            pe.wait_ge(x_loaded, 16 * SB)
            def flip_x(v):
                if isinstance(v, int):
                    pe.wait_ge(small_loaded, 16 * 12)
                    pe.wait_ge(weights_zeroed, 2)
                flip(v, flip_hop1(v))

            finish_last = product(HOP1, x0, None, finish_hop1, [(REAR - BPS, False, flip_x)])

            def finish_hop2(v):
                sums_ready(HOP2, v)
                pe.wait_ge(flip_read, flip_hop2(v) + 1)
                project(pe_rows, [(sums, W_H2A), (paired, W_H2X)], rows_hop2(v))

            def gcn_flip(v):
                flip(5 + 2 * v, flip_gcn(v))

            def gcn_rows(v):
                pe.wait_ge(flip_read, flip_gcn(v) + 1)
                project(pe_rows, [(paired, W_GCN)], rows_gcn(v))

            finish_last = product(HOP2, hop, (rows_read, rows_hop1(0)), finish_hop2,
                    [(REAR - 4, True, lambda v: gcn_flip(v - 1)), (REAR - 3, True, lambda v: gcn_rows(v - 1)),
                     (REAR - 2, False, lambda v: flip(4 + 2 * v, flip_hop2(v)))], finish_last)
            finish_last()
            gcn_flip(SB - 1)
            gcn_rows(SB - 1)

            pe.wait_ge(rows_read, rows_spread(0))
            pe.wait_ge(evacuated, pe_no(CHEB1, 0, 0) + TURN_BUFS)
            for v in range(SB):
                s = superblock(SPREAD, v)
                for q in quarters(SPREAD):
                    pe.wait_ge(chunk_loaded[q], loaded(SPREAD, v, q))
                    for t in range(BPS):
                        columns = ring[:, q, t, :].rearrange("k (p m) -> k m p", m=BPS)
                        for half in range(2):
                            ins = pe.matmul(pe_turn[q // 2][F * half:F * half + F, q % 2, :],
                                            z[:, BPS * s + t, :], columns[:, half * (BPS // 2):(half + 1) * (BPS // 2), :],
                                            start=(v == 0 and t == 0), stop=(v == SB - 1 and t == BPS - 1),
                                            skip_group_check=True)
                    ins.then_inc(spread, 1)

            def spread_rows(q):
                pe.wait_ge(spread_copied, q + 1)
                for t in range(BPS // 2):
                    pe.matmul(pairs(t)(spread_bank(q)), spread_sums[:, q, t * P:(t + 1) * P],
                              wb[:, W_ONE, :].rearrange("p (h f) -> p h f", h=2), start=True, stop=False)
                    ins = pe.matmul(pairs(t)(spread_bank(q)), ident[:, :], pairs(t)(z[:, q * BPS:(q + 1) * BPS, :]),
                                    start=False, stop=True)
                ins.then_inc(rows_filled, 1)

            for q in range(SB):
                spread_rows(q)

            def finish_cheb1(v):
                sums_ready(CHEB1, v)
                project(pe_rows, [(sums, W_ONE)], rows_cheb1(v))
                pe.wait_ge(flip_read, flip_cheb1(v) + 1)
                project(pe_flip, [(sums, W_C1), (paired, W_C0)], filt_cheb1(v))

            pe.wait_ge(rows_read, rows_spread(SB - 1) + 1)
            finish_last = product(CHEB1, y2, (y2_ready, 0), finish_cheb1, [(REAR - BPS + 2, False, lambda v: flip(12 + v, flip_cheb1(v)))])

            def finish_cheb2(v):
                sums_ready(CHEB2, v)
                project(pe_rows, [(sums, W_ONE)], rows_cheb2(v))
                project(pe_flip, [(sums, W_C2)], filt_cheb2(v))

            finish_last = product(CHEB2, t1, (rows_read, rows_cheb1(0)), finish_cheb2, (), finish_last)

            def finish_cheb3(v):
                sums_ready(CHEB3, v)
                project(pe_flip, [(sums, W_C3)], filt_cheb3(v))

            def gat_flip(v):
                flip(16 + v, flip_gat(v))

            def gat_rows(v):
                pe.wait_ge(flip_read, flip_gat(v) + 1)
                project(pe_rows, [(paired, W_GAT)], rows_gat(v))

            finish_last = product(CHEB3, t2, (rows_read, rows_cheb2(0)), finish_cheb3,
                    [(REAR - 4, True, lambda v: gat_flip(v - 1)), (REAR - 3, True, lambda v: gat_rows(v - 1))], finish_last)
            finish_last()
            gat_flip(SB - 1)
            gat_rows(SB - 1)

            pe.wait_ge(verdict_ready, 1)
            one = pe.value_load(onehot[0:1, 0:1], min_val=0, max_val=1)
            with pe.If(one == 0):
                pe.wait_ge(in_order, 16 * 3)
                for c in range(2):
                    ins = pe.transpose(pe_turn[0][:, 0, c * P:(c + 1) * P],
                                       att[:, 1, c * 16:(c + 1) * 16, :].rearrange("p b h -> p (b h)"), ident[:, :])
                ins.then_inc(neigh_turned, 1)
                pe.wait_ge(neigh_copied, 1)
                for g in range(2):
                    with pe.Fori(0, BLOCKS) as b:
                        pe.wait_ge(heads_read, b + (g * BLOCKS + 1))
                        for h in range(4):
                            first = 4 * BLOCKS * g + h
                            pe.wait_ge(probs_ready, b * 4 + (first + 2))
                            for c in range(9):
                                if c < 8:
                                    if c >= 2:
                                        pe.wait_ge(probs_copied, b * 32 + (8 * first + c))
                                    else:
                                        pe.wait_ge(probs_copied, b * 32 + (8 * first + 1))
                                    for t in range(4):
                                        ins = pe.transpose(pe_turn[c % 2][:, 0, t * P:(t + 1) * P],
                                                           probs()[:, (4 * c + t) * P:(4 * c + t + 1) * P], ident[:, :])
                                    ins.then_inc(probs_turned, 1)
                                if c >= 1:
                                    pe.wait_ge(probs_copied, b * 32 + (8 * first + c + 1))
                                    for t in range(4):
                                        j = 4 * (c - 1) + t
                                        head = (4 * g + h) * D
                                        ins = pe.matmul(pe_sum[:, h * D:(h + 1) * D],
                                                        tiles[:, (c - 1) % TILE_BUFS, t * P:(t + 1) * P],
                                                        feats[:, j, head:head + D],
                                                        start=(j == 0), stop=(j == BLOCKS - 1))
                            ins.then_inc(heads_summed, 1)
            pe.wait_ge(verdict_ready, 1)

        @block.scalar
        def _(act):
            for source, w, k in wb_loads:
                for half in range(2):
                    act.dma_start(wb[F * half:F * half + F, w:w + k, F * half:F * half + F], source)\
                        .then_inc(small_loaded, 16)
            for i, source in enumerate(rows_loads):
                act.dma_start(per_row[:, i, :], source.partition_broadcast(P)).then_inc(small_loaded, 16)

            def visit(stream, v, finish):
                for pos in range(STEPS):
                    block = quarters(stream)[pos // BPS] * BPS + pos % BPS
                    if pos in BY_PE:
                        act.wait_ge(pe_turned, pe_no(stream, v, pos) + 1)
                        before = pos - TURN_BUFS if pos >= BY_PE[TURN_BUFS] else -1
                        act.wait_ge(multiplied, step_no(stream, v, before) + 1 + TILE_BUFS)
                        tile = pe_tiles[:, pos % TURN_BUFS, :]
                        source = pe_turn[pos % TURN_BUFS][:, :, :].rearrange("p a n -> p (a n)")
                        if stream == HOP1:
                            act.activation(tile, source, ACT.Copy, accum_out=deg_part[:, block:block + 1])\
                                .then_inc(evacuated, 1)
                        else:
                            act.activation(tile, source, ACT.Copy).then_inc(evacuated, 1)
                    elif stream == HOP1:
                        act.wait_ge(dve_turned, dve_no(stream, v, pos) + 1)
                        if pos == 0:
                            act.wait_ge(deg_added, v)
                        if pos > 0 or not isinstance(v, int):
                            act.wait_ge(degrees_taken, dve_no(stream, v, pos))
                        tile = tiles[:, pos % TILE_BUFS, :]
                        act.activation(spare[:, :, :].rearrange("p b f -> p (b f)"), tile, ACT.Copy,
                                       accum_out=deg_part[:, block:block + 1]).then_inc(degrees_taken, 1)
                    if pos == 1 and not isinstance(v, int):
                        finish(v - 1)
                act.wait_ge(multiplied, step_no(stream, v, STEPS - 1) + 1 + TILE_BUFS)
                act.activation(sums[:, :], pe_sum[:, :], ACT.Copy).then_inc(sums_copied, 1)

            def product(stream, finish):
                visit(stream, 0, finish)
                with act.Fori(1, SB) as v:
                    visit(stream, v, finish)
                finish(SB - 1)

            def finish_hop1(v):
                act.wait_ge(rows_filled, rows_hop1(v) + 1)
                act.activation(rows_of(hop, superblock(HOP1, v)), pe_rows[:, :, :], ACT.Tanh).then_inc(rows_read, 1)

            def finish_hop2(v):
                act.wait_ge(rows_filled, rows_hop2(v) + 1)
                act.activation(second_hop[:, :, :], pe_rows[:, :, :], ACT.Tanh).then_inc(rows_read, 1)

            def finish_cheb1(v):
                act.wait_ge(rows_filled, rows_cheb1(v) + 1)
                act.activation(rows_of(t1, superblock(CHEB1, v)), pe_rows[:, :, :], ACT.Copy).then_inc(rows_read, 1)

            product(HOP1, finish_hop1)
            product(HOP2, finish_hop2)

            def far_search(v):
                for q in range(NATURAL):
                    i = far_no(v, q)
                    first = isinstance(v, int) and v == 0 and q == 0
                    act.wait_ge(far_found, i + 1)
                    if not first:
                        act.wait_ge(far_summed, FAR * i)
                    for t in range(FAR):
                        act.activation(far_tiles[t], ring[:, q, NEAR + t, :], ACT.Sign,
                                       bias=far8[:, t, 0:1], scale=-1.0).then_inc(compared, 1)
                    for t in range(FAR):
                        act.wait_ge(numbered, FAR * i + t + 1)
                        if t == 0 and not first:
                            act.wait_ge(far_taken, i)
                        act.activation(far_tiles[t], far_tiles[t], ACT.Copy,
                                       accum_out=far_sum[:, t:t + 1]).then_inc(far_summed, 1)

            far_search(0)
            with act.Fori(1, SB) as v:
                far_search(v)
            act.wait_ge(spread, SB * SB)
            for q in range(SB):
                act.activation(spread_sums[:, q, :], pe_turn[q // 2][:, q % 2, :], ACT.Copy).then_inc(spread_copied, 1)
            product(CHEB1, finish_cheb1)
            product(CHEB2, lambda v: None)
            product(CHEB3, lambda v: None)

            act.wait_ge(verdict_ready, 1)
            one = act.value_load(onehot[0:1, 0:1], min_val=0, max_val=1)
            with act.If(one == 0):
                for g in range(2):
                    with act.Fori(0, BLOCKS) as b:
                        for h in range(4):
                            first = 4 * BLOCKS * g + h
                            act.wait_ge(scores_ready, b * 4 + first + 1)
                            act.wait_ge(probs_turned, b * 32 + (8 * first + 1))
                            act.activation(probs(), scores(), ACT.Exp, bias=neg_max[:, h:h + 1],
                                           accum_out=weight_sum[:, h:h + 1]).then_inc(probs_ready, 1)
                            for c in range(8):
                                act.wait_ge(probs_turned, b * 32 + (8 * first + c + 2))
                                act.activation(tiles[:, c % TILE_BUFS, 0:HALF], pe_turn[c % 2][:, 0, :], ACT.Copy)\
                                    .then_inc(probs_copied, 1)
            act.wait_ge(verdict_ready, 1)

        @block.vector
        def _(dve):
            links = {"before": 0, "here": 0}
            loop = []

            def mark(ins):
                ins.then_inc(vec, 1)
                links["here"] += 1

            def join(apart=False):
                count = links["before"] + links["here"]
                if loop:
                    var, start, per = loop[0]
                    count = var * per + (count - start * per)
                if apart:
                    wait_apart(dve, vec, count, consts_zeroed)
                else:
                    dve.wait_ge(vec, count)

            def link(ins):
                mark(ins)
                join()

            def enter(var, start, per):
                links["before"] += links["here"]
                links["here"] = 0
                loop.append((var, start, per))

            def leave(turns):
                per = loop.pop()[2]
                assert links["here"] == per, f"a turn of the loop has {links['here']} links, not {per}"
                links["before"] += per * turns
                links["here"] = 0

            def inverse_root(y, v_in, t):
                link(dve.tensor_scalar(t.bitcast(U32), v_in.bitcast(U32), 1, None, ALU.logical_shift_right))
                link(dve.tensor_scalar(y.bitcast(I32), t.bitcast(I32), -1.0, float(0x5F3759DF), ALU.mult, ALU.add))
                for _ in range(3):
                    link(dve.tensor_tensor(t, y, y, ALU.mult))
                    link(dve.scalar_tensor_tensor(t, t, -0.5, v_in, ALU.mult, ALU.mult))
                    link(dve.scalar_tensor_tensor(y, t, 1.5, y, ALU.add, ALU.mult))

            def wide(a):
                return a.unsqueeze(2).to_broadcast([P, BPS, F])

            def for_all(i):
                return per_row[:, i, :].unsqueeze(1).to_broadcast([P, BPS, F])

            def norm(final):
                link(dve.tensor_reduce(rowsum[:, :], work[:, :, :], X, ALU.add))
                link(dve.scalar_tensor_tensor(work[:, :, :], wide(rowsum[:, :]), -1.0 / F, work[:, :, :],
                                              ALU.mult, ALU.add))
                link(dve.tensor_tensor(square[:, :, :], work[:, :, :], work[:, :, :], ALU.mult))
                link(dve.tensor_reduce(rowsum[:, :], square[:, :, :], X, ALU.add))
                v = root_x[:, 0:BPS]
                link(dve.tensor_scalar(v, rowsum[:, :], 1.0 / F, EPS, ALU.mult, ALU.add))
                inverse_root(root_y[:, 0:BPS], v, root_t[:, 0:BPS])
                final(work[:, :, :], wide(root_y[:, 0:BPS]))

            def scan(stream, v, q, half):
                base, count = (0, NEAR) if stream == SPREAD else (SCAN * half, SCAN)
                s = superblock(stream, v)
                wait_apart(dve, chunk_loaded[q], loaded(stream, v, q), consts_zeroed)
                for t in range(count):
                    ins = dve.max(top8[:, t, :], ring[:, q, base + t, :])
                mark(ins)
                join(apart=True)
                for t in range(count):
                    ins = dve.max_index(top8_at[:, t, :], top8[:, t, :], ring[:, q, base + t, :])
                ins.then_inc(scanned, 1)
                wait_apart(dve, scanned, scan_no(stream, v, q, half) + 1, consts_zeroed)
                mark(dve.tensor_copy(top2[:, bass.ds(s * BPS + base, count), q, :], top8[:, 0:count, 0:2]))
                mark(dve.tensor_copy(top_at[:, bass.ds(s * BPS + base, count), q], top8_at[:, 0:count, 0]))
                join(apart=True)

            def turn(stream, v, steps):
                for pos in steps:
                    q, j = quarters(stream)[pos // BPS], pos % BPS
                    if j == 0:
                        dve.wait_ge(chunk_loaded[q], loaded(stream, v, q))
                    opening = isinstance(v, int) and v == 0 and pos < TILE_BUFS
                    if not (stream == HOP1 and opening):
                        dve.wait_ge(multiplied, user_before(stream, v, pos) + 1 + TILE_BUFS)
                        if stream == HOP1 or (stream == HOP2 and opening):
                            dve.wait_ge(degrees_taken, dve_no(stream, v, pos) - TILE_BUFS + 1)
                    dve.transpose(tiles[:, pos % TILE_BUFS, :], ring_runs[:, q, :, j::BPS]).then_inc(dve_turned, 1)

            def stage(buf, s):
                dve.tensor_copy(staged_by_half(), split(rows_of(buf, s))).then_inc(staged, 1)

            def take_flip(count):
                dve.wait_ge(flip_filled, count + 1)
                source = pe_flip[:, :, :].rearrange("p b f -> p (b f)")
                dve.tensor_copy(paired[:, :], source).then_inc(flip_read, 1)

            def visits(stream, before, other, peel, per, done=0):
                def body(v):
                    turn(stream, v, range(done if isinstance(v, int) and v == 0 else 0, BPS))
                    if isinstance(v, int) and v == 0:
                        before()
                    turn(stream, v, range(BPS, BY_PE[0]))
                    rear = BY_PE[-1] + 1 if stream in (HOP1, CHEB1, CHEB2) else REAR
                    turn(stream, v, range(BY_PE[-1] + 1, rear))
                    other(v)
                    turn(stream, v, range(rear, STEPS))
                    if stream == HOP1:
                        add_degrees(v)

                for v in range(peel):
                    body(v)
                with dve.Fori(peel, SB) as v:
                    enter(v, peel, per)
                    body(v)
                    leave(SB - peel)

            def filter_weights():
                dve.wait_ge(small_loaded, 16 * 12)
                dve.wait_ge(weights_zeroed, 2)
                mark(dve.tensor_tensor(wb[:, W_C0, :], wb[:, W_C0, :], wb[:, W_C2, :], ALU.subtract))
                link(dve.tensor_tensor(wb[:, W_C1, :], wb[:, W_C1, :], wb[:, W_C3, :], ALU.subtract))
                link(dve.tensor_scalar(wb[:, W_C2:W_C3 + 1, :], wb[:, W_C2:W_C3 + 1, :], 2.0, None, ALU.mult))

            def hop1(v):
                if isinstance(v, int):
                    dve.wait_ge(x_loaded, 16 * SB)
                stage(x0, superblock(HOP1, v))
                scan(HOP1, v, NATURAL, 0)
                take_flip(flip_hop1(v))

            def add_degrees(v):
                dve.wait_ge(evacuated, pe_no(HOP1, v, BPS - 1) + 1 + TURN_BUFS)
                dve.wait_ge(degrees_taken, dve_no(HOP1, v, STEPS - 1) + 1)
                dve.tensor_tensor(deg[:, :], deg[:, :], deg_part[:, :], ALU.add).then_inc(deg_added, 1)
                dve.wait_ge(deg_added, v + 1)

            for half in range(2):
                dve.memset(wb[F * half:F * half + F, 0:W_ONE, F - F * half:2 * F - F * half], 0.0)\
                    .then_inc(weights_zeroed, 1)
            dve.wait_ge(consts_zeroed, 3)
            visits(HOP1, lambda: None, hop1, 1, 3)

            def scales_and_weights():
                link(dve.tensor_scalar(root_x[:, :], deg[:, :], 1e-30, None, ALU.max))
                inverse_root(root_y[:, :], root_x[:, :], root_t[:, :])
                link(dve.tensor_scalar(root_t[:, :], deg[:, :], 0.0, None, ALU.is_gt))
                link(dve.tensor_tensor(dinv[:, :], root_y[:, :], root_t[:, :], ALU.mult))
                filter_weights()

            def norm_hop2(v):
                s = superblock(HOP2, v)
                wait_apart(dve, rows_read, rows_hop2(v) + 1, consts_zeroed)
                link(dve.tensor_tensor(work[:, :, :], second_hop[:, :, :], rows_of(x0, s), ALU.add))
                norm(lambda rows, factor: dve.tensor_tensor(staged_by_half(), split(rows), split(factor), ALU.mult)
                     .then_inc(staged, 1))
                dve.wait_ge(staged, 6 + 2 * v)
                link(dve.tensor_copy(split(rows_of(y1, s)), staged_by_half()))

            def scale_z(v):
                s = superblock(HOP2, v)
                wait_apart(dve, rows_filled, rows_gcn(v) + 1, consts_zeroed)
                factor = dinv[:, bass.ds(s * BPS, BPS)].unsqueeze(2).to_broadcast([P, BPS, F])
                dve.tensor_tensor(rows_of(z, s), pe_rows[:, :, :], factor, ALU.mult).then_inc(rows_read, 1)

            def hop2(v):
                if isinstance(v, int) and v == 0:
                    scales_and_weights()
                    dve.wait_ge(rows_read, rows_hop1(SB - 1) + 1)
                else:
                    norm_hop2(v - 1)
                    take_flip(flip_gcn(v - 1))
                    scale_z(v - 1)
                stage(hop, superblock(HOP2, v))
                take_flip(flip_hop2(v))

            visits(HOP2, lambda: None, hop2, 1, 18)
            norm_hop2(SB - 1)
            take_flip(flip_gcn(SB - 1))
            scale_z(SB - 1)

            def far_maxima(v, q):
                s = superblock(SPREAD, v)
                i = far_no(v, q)
                wait_apart(dve, chunk_loaded[q], loaded(SPREAD, v, q), consts_zeroed)
                if not (isinstance(v, int) and i == 0):
                    wait_apart(dve, compared, FAR * i, consts_zeroed)
                for t in range(FAR):
                    ins = dve.max(far8[:, t, :], ring[:, q, NEAR + t, :])
                ins.then_inc(far_found, 1)
                wait_apart(dve, far_found, i + 1, consts_zeroed)
                mark(dve.tensor_copy(top2[:, bass.ds(s * BPS + NEAR, FAR), q, :], far8[:, :, 0:2]))
                join(apart=True)

            def far_places(v, q):
                s = superblock(SPREAD, v)
                wait_apart(dve, far_summed, FAR * (far_no(v, q) + 1), consts_zeroed)
                dve.tensor_copy(top_at[:, bass.ds(s * BPS + NEAR, FAR), q], far_sum).then_inc(far_taken, 1)

            def search(v):
                for q in range(NATURAL):
                    far_maxima(v, q)
                    if q > 0:
                        far_places(v, q - 1)
                    elif not isinstance(v, int):
                        far_places(v - 1, NATURAL - 1)
                    scan(SPREAD, v, q, 0)

            search(0)
            with dve.Fori(1, SB) as v:
                enter(v, 1, 12)
                search(v)
                leave(SB - 1)
            far_places(SB - 1, NATURAL - 1)

            turn(CHEB1, 0, range(TILE_BUFS))

            for q in range(SB):
                blocks = slice(q * BPS, (q + 1) * BPS)
                dve.wait_ge(rows_filled, rows_spread(q) + 1)
                dve.tensor_tensor(y2[:, blocks, :], spread_bank(q), wide(dinv[:, blocks]), ALU.mult)\
                    .then_inc(rows_read, 1)
            dve.wait_ge(rows_read, rows_spread(SB - 1) + 1)

            def wide_all(a):
                return a.unsqueeze(2).to_broadcast([P, BLOCKS, F])

            link(dve.tensor_tensor(y2[:, :, :], y2[:, :, :], per_row[:, 0, :].unsqueeze(1).to_broadcast([P, BLOCKS, F]), ALU.add))
            link(dve.scalar_tensor_tensor(y2[:, :, :], y2[:, :, :], 0.0, y1[:, :, :], ALU.max, ALU.add))
            squares = buf_b
            link(dve.tensor_reduce(root_t[:, :], y2[:, :, :], X, ALU.add))
            link(dve.scalar_tensor_tensor(y2[:, :, :], wide_all(root_t[:, :]), -1.0 / F, y2[:, :, :], ALU.mult, ALU.add))
            link(dve.tensor_tensor(squares[:, :, :], y2[:, :, :], y2[:, :, :], ALU.mult))
            link(dve.tensor_reduce(root_x[:, :], squares[:, :, :], X, ALU.add))
            link(dve.tensor_scalar(root_x[:, :], root_x[:, :], 1.0 / F, EPS, ALU.mult, ALU.add))
            inverse_root(root_y[:, :], root_x[:, :], root_t[:, :])
            for q in range(SB):
                blocks = slice(q * BPS, (q + 1) * BPS)
                dve.tensor_tensor(y2[:, blocks, :], y2[:, blocks, :], wide(root_y[:, blocks]), ALU.mult)\
                    .then_inc(y2_ready, 1)
            dve.wait_ge(y2_ready, SB)

            def find_leads():
                dve.wait_ge(far_taken, far_no(SB, 0))
                far = top_at[:, :, :].rearrange("p (s m) q -> p s m q", s=SB)[:, :, NEAR:BPS, 0:NATURAL]
                link(dve.tensor_scalar(far, far, -1.0, float(QUARTER * (QUARTER - 1) // 2), ALU.mult, ALU.add))
                for b in range(BLOCKS):
                    ins = dve.max(best[:, b, :], top2[:, b, :, :].rearrange("p q k -> p (q k)"))
                link(ins)
                largest = best[:, :, 0:1].to_broadcast([P, BLOCKS, SB])
                for q in range(SB):
                    mark(dve.tensor_scalar(top_at[:, :, q], top_at[:, :, q], float(q * QUARTER), None, ALU.add))
                link(dve.tensor_tensor(hit[:, :, :], top2[:, :, :, 0], largest, ALU.is_equal))
                link(dve.tensor_tensor(hit[:, :, :], hit[:, :, :], top_at[:, :, :], ALU.mult))
                link(dve.tensor_reduce(neighbour[:, :], hit[:, :, :], X, ALU.add))
                link(dve.tensor_copy(neighbour_u[:, :], neighbour[:, :]))
                for k in range(2):
                    link(dve.tensor_scalar(lead[:, k, :], best[:, :, k], -1.0, 1.0, ALU.mult, ALU.add))
                    link(dve.tensor_scalar(lead[:, k, :], lead[:, k, :], NEG, None, ALU.mult))
                link(dve.tensor_tensor(lead[:, 1, :], lead[:, 1, :], lead[:, 0, :], ALU.subtract))
                link(dve.tensor_scalar(lead[:, 2, :], lead[:, 0, :], 2.0 ** -20, None, ALU.mult))
                link(dve.scalar_tensor_tensor(lead[:, 2, :], lead[:, 2, :], -1.0, lead[:, 2, :], ALU.mult, ALU.max))
                link(dve.scalar_tensor_tensor(lead[:, 2, :], lead[:, 1, :], 0.99, lead[:, 2, :], ALU.mult, ALU.add))
                link(dve.tensor_reduce(worst[:, 0:1], lead[:, 2, :], X, ALU.max))

            def keep_cheb1(v):
                wait_apart(dve, flip_filled, filt_cheb1(v) + 1, consts_zeroed)
                dve.tensor_copy(rows_of(filtered, superblock(CHEB1, v)), pe_flip[:, :, :]).then_inc(flip_read, 1)

            def cheb1(v):
                first = isinstance(v, int) and v == 0
                if not first:
                    keep_cheb1(v - 1)
                stage(y2, superblock(CHEB1, v))
                scan(CHEB1, v, NATURAL, 1)
                take_flip(flip_cheb1(v))

            visits(CHEB1, lambda: None, cheb1, 1, 3, TILE_BUFS)

            def after_cheb1():
                keep_cheb1(SB - 1)
                dve.wait_ge(flip_read, filt_cheb1(SB - 1) + 1)

            def keep_cheb2(v):
                s = superblock(CHEB2, v)
                wait_apart(dve, rows_filled, rows_cheb2(v) + 1, consts_zeroed)
                dve.scalar_tensor_tensor(rows_of(t2, s), pe_rows[:, :, :], 2.0, rows_of(y2, s),
                                         ALU.mult, ALU.subtract).then_inc(rows_read, 1)
                wait_apart(dve, flip_filled, filt_cheb2(v) + 1, consts_zeroed)
                dve.tensor_tensor(rows_of(filtered, s), rows_of(filtered, s), pe_flip[:, :, :], ALU.add)\
                    .then_inc(flip_read, 1)

            def cheb2(v):
                if isinstance(v, int) and v == 0:
                    find_leads()
                else:
                    keep_cheb2(v - 1)

            visits(CHEB2, after_cheb1, cheb2, 1, 0)

            def after_cheb2():
                keep_cheb2(SB - 1)
                dve.wait_ge(flip_read, filt_cheb2(SB - 1) + 1)

            def norm_cheb3(v):
                s = superblock(CHEB3, v)
                wait_apart(dve, flip_filled, filt_cheb3(v) + 1, consts_zeroed)
                dve.tensor_tensor(work[:, :, :], rows_of(filtered, s), pe_flip[:, :, :], ALU.add).then_inc(flip_read, 1)
                dve.wait_ge(flip_read, filt_cheb3(v) + 1)
                link(dve.tensor_tensor(work[:, :, :], work[:, :, :], rows_of(y2, s), ALU.add))
                norm(lambda rows, factor: dve.tensor_tensor(staged_by_half(), split(rows), split(factor), ALU.mult)
                     .then_inc(staged, 1))
                dve.wait_ge(staged, 17 + v)
                link(dve.tensor_copy(split(rows_of(y3, s)), staged_by_half()))
                take_flip(flip_gat(v))
                wait_apart(dve, rows_filled, rows_gat(v) + 1, consts_zeroed)
                dve.tensor_copy(rows_of(feats, s), pe_rows[:, :, :]).then_inc(rows_read, 1)
                dve.wait_ge(rows_read, rows_gat(v) + 1)
                for i in range(2):
                    link(dve.tensor_tensor(square[:, :, :], rows_of(feats, s), for_all(1 + i), ALU.mult))
                    link(dve.tensor_reduce(att[:, i, bass.ds(s * BPS, BPS), :],
                                           square[:, :, :].rearrange("p b (h d) -> p b h d", h=H), X, ALU.add))

            def cheb3(v):
                if not (isinstance(v, int) and v == 0):
                    norm_cheb3(v - 1)

            visits(CHEB3, after_cheb2, cheb3, 1, 22)
            norm_cheb3(SB - 1)

            for i in range(2):
                att_i = att[:, i, :, :].rearrange("p b h -> p (b h)")
                ins = dve.tensor_reduce(worst[:, 1 + i:2 + i], att_i, X, ALU.max, apply_absolute_value=True)
            ins.then_inc(worst_found, 1)
            dve.wait_ge(worst_reduced, 1)
            link(dve.tensor_tensor(verdict[:, 0:1], worst_all[:, 1:2], worst_all[:, 2:3], ALU.add))
            link(dve.tensor_scalar(verdict[:, 0:1], verdict[:, 0:1], 2.0, 128.0, ALU.mult, ALU.add))
            link(dve.tensor_tensor(verdict[:, 1:2], verdict[:, 0:1], worst_all[:, 0:1], ALU.add))
            dve.tensor_scalar(onehot[:, :], verdict[:, 1:2], 0.0, None, ALU.is_lt).then_inc(verdict_ready, 1)
            dve.wait_ge(verdict_ready, 1)
            one = dve.value_load(onehot[0:1, 0:1], min_val=0, max_val=1)

            def last_norm(s):
                blocks = slice(s * BPS, (s + 1) * BPS)
                dve.wait_ge(out_ready, s)
                link(dve.tensor_tensor(work[:, :, :], attended[:, blocks, :], for_all(3), ALU.add))
                link(dve.scalar_tensor_tensor(work[:, :, :], work[:, :, :], 0.0, y3[:, blocks, :], ALU.max, ALU.add))
                norm(lambda rows, factor: dve.tensor_tensor(attended[:, blocks, :], rows, factor, ALU.mult)
                     .then_inc(out_ready, 1))

            taken = links["before"] + links["here"]
            with dve.If(one == 1):
                for s in range(SB):
                    dve.wait_ge(gathered[s], 16 * BPS)
                    last_norm(s)
            links.update(before=taken, here=0)
            with dve.Else():
                dve.wait_ge(neigh_turned, 1)
                dve.tensor_copy(staged_rows[:, :, :].rearrange("p b f -> p (b f)")[:, 0:2 * P],
                                pe_turn[0][:, 0, 0:2 * P]).then_inc(neigh_copied, 1)
                for g in range(2):
                    dve.wait_ge(neigh_loaded, 64 * (g + 1))
                    with dve.Fori(0, BLOCKS) as b:
                        enter(b, 0, 19)
                        dve.wait_ge(mask_loaded, b * 16 + (g * BLOCKS + 1) * 16)
                        link(dve.tensor_scalar(mask(), mask(), -1.0, 1.0, ALU.mult, ALU.add))
                        link(dve.tensor_scalar(mask(), mask(), NEG, None, ALU.mult))
                        for h in range(4):
                            head = 4 * g + h
                            first = 4 * BLOCKS * g + h
                            dve.wait_ge(probs_ready, b * 4 + (first + 1))
                            link(dve.tensor_scalar(scores(), neigh_terms(h), att[:, 0, bass.ds(b, 1), head],
                                                   None, ALU.add))
                            link(dve.scalar_tensor_tensor(scores(), scores(), 0.2, scores(), ALU.mult, ALU.max))
                            link(dve.tensor_tensor(scores(), scores(), mask(), ALU.add))
                            link(dve.tensor_reduce(neg_max[:, h:h + 1], scores(), X, ALU.max))
                            dve.tensor_scalar(neg_max[:, h:h + 1], neg_max[:, h:h + 1], -1.0, None, ALU.mult)\
                                .then_inc(scores_ready, 1)
                        dve.wait_ge(heads_summed, b * 4 + (4 * BLOCKS * g + 4))
                        link(dve.reciprocal(weight_sum[:, :], weight_sum[:, :]))
                        dst = attended[:, bass.ds(b, 1), 4 * g * D:4 * (g + 1) * D].rearrange("p b (h d) -> p (b h) d", h=4)
                        dve.tensor_tensor(dst, pe_sum[:, 0:4 * D].rearrange("p (h d) -> p h d", h=4),
                                                 weight_sum[:, :].unsqueeze(2).to_broadcast([P, 4, D]), ALU.mult)\
                            .then_inc(heads_read, 1)
                        leave(BLOCKS)
                dve.wait_ge(attended_back, 16 * SB)
                for s in range(SB):
                    last_norm(s)
            dve.wait_ge(verdict_ready, 1)


_INS = ['x', 'adj', 'L0_gnn_W', 'L1_gnn_W', 'L1_gnn_b', 'L2_gnn_weight', 'L3_gnn_W',
        'L3_gnn_att_self', 'L3_gnn_att_neigh', 'L3_gnn_bias']
_OUTS = [((4096, 64), 'float32')]


def kernel(**inputs):
    import numpy as _np
    import concourse.bacc as _bacc
    from concourse import mybir as _mybir
    from concourse.bass_utils import run_bass_kernel_spmd as _run

    nc = _bacc.Bacc("TRN2", target_bir_lowering=False, num_devices=1)
    arrays, args = {}, []
    for name in _INS:
        a = _np.ascontiguousarray(inputs[name])
        arrays[f"in_{name}_dram"] = a
        args.append(nc.dram_tensor(f"in_{name}_dram", a.shape, _mybir.dt.from_np(a.dtype), kind="ExternalInput").ap())
    for i, (shape, dtype) in enumerate(_OUTS):
        dt = _mybir.dt.from_np(_np.dtype(dtype))
        args.append(nc.dram_tensor(f"out_{i}_dram", shape, dt, kind="ExternalOutput").ap())
    build(nc, *args)
    r = _run(nc, [arrays], core_ids=[0])
    return r.results[0]["out_0_dram"]
```
